# Optimizing a Trainium2 kernel written in Bass

```python
import numpy as np
import jax
import jax.numpy as jnp

def _softmax(x, axis=-1):
    return jax.nn.softmax(x, axis=axis)

def _gelu(x):
    return jax.nn.gelu(x, approximate=True)

def _silu(x):
    return jax.nn.silu(x)

def _sigmoid(x):
    return jax.nn.sigmoid(x)

def _layernorm(x, axis=-1, eps=1e-05):
    m = jnp.mean(x, axis=axis, keepdims=True)
    v = jnp.var(x, axis=axis, keepdims=True)
    return (x - m) / jnp.sqrt(v + eps)

def _scatter_add(tgt, idx, src, axis=0):
    return tgt.at[idx].add(src)

def _segment_sum(src, seg, n):
    return jax.ops.segment_sum(src, seg, n)
kernel_name = 'mk_dlrm_tower_d1_rec_r8_7f5029'

def setup_inputs(seed: int=0):
    np.random.seed(seed)
    _w = jnp.asarray

    def _rec_inputs():
        import jax
        import jax.numpy as jnp
        _tk = jax.random.key(seed)
        dense_ctx = jax.random.normal(jax.random.fold_in(_tk, 190), (512, 16), jnp.float32)
        ids = jnp.stack([jax.random.randint(jax.random.fold_in(_tk, 200 + f), (512,), 0, v, jnp.int32) for f, v in enumerate([125000, 1000, 1250, 1000, 1250, 1250, 12500, 1250, 1250, 125000, 1250, 12500, 1250, 12500, 12500, 125000, 1250, 1000, 125000, 125000, 1250, 1250, 12500, 1250, 1000, 12500, 1000, 12500, 1000, 125000, 1000, 12500, 1250, 1250, 1000, 1250, 12500, 12500, 1000])], axis=1)
        tbl_0 = 0.05 * jax.random.normal(jax.random.fold_in(_tk, 500 + 0), (125000, 32), jnp.float32)
        tbl_1 = 0.05 * jax.random.normal(jax.random.fold_in(_tk, 500 + 1), (1000, 32), jnp.float32)
        tbl_2 = 0.05 * jax.random.normal(jax.random.fold_in(_tk, 500 + 2), (1250, 32), jnp.float32)
        tbl_3 = 0.05 * jax.random.normal(jax.random.fold_in(_tk, 500 + 3), (1000, 32), jnp.float32)
        tbl_4 = 0.05 * jax.random.normal(jax.random.fold_in(_tk, 500 + 4), (1250, 32), jnp.float32)
        tbl_5 = 0.05 * jax.random.normal(jax.random.fold_in(_tk, 500 + 5), (1250, 32), jnp.float32)
        tbl_6 = 0.05 * jax.random.normal(jax.random.fold_in(_tk, 500 + 6), (12500, 32), jnp.float32)
        tbl_7 = 0.05 * jax.random.normal(jax.random.fold_in(_tk, 500 + 7), (1250, 32), jnp.float32)
        tbl_8 = 0.05 * jax.random.normal(jax.random.fold_in(_tk, 500 + 8), (1250, 32), jnp.float32)
        tbl_9 = 0.05 * jax.random.normal(jax.random.fold_in(_tk, 500 + 9), (125000, 32), jnp.float32)
        tbl_10 = 0.05 * jax.random.normal(jax.random.fold_in(_tk, 500 + 10), (1250, 32), jnp.float32)
        tbl_11 = 0.05 * jax.random.normal(jax.random.fold_in(_tk, 500 + 11), (12500, 32), jnp.float32)
        tbl_12 = 0.05 * jax.random.normal(jax.random.fold_in(_tk, 500 + 12), (1250, 32), jnp.float32)
        tbl_13 = 0.05 * jax.random.normal(jax.random.fold_in(_tk, 500 + 13), (12500, 32), jnp.float32)
        tbl_14 = 0.05 * jax.random.normal(jax.random.fold_in(_tk, 500 + 14), (12500, 32), jnp.float32)
        tbl_15 = 0.05 * jax.random.normal(jax.random.fold_in(_tk, 500 + 15), (125000, 32), jnp.float32)
        tbl_16 = 0.05 * jax.random.normal(jax.random.fold_in(_tk, 500 + 16), (1250, 32), jnp.float32)
        tbl_17 = 0.05 * jax.random.normal(jax.random.fold_in(_tk, 500 + 17), (1000, 32), jnp.float32)
        tbl_18 = 0.05 * jax.random.normal(jax.random.fold_in(_tk, 500 + 18), (125000, 32), jnp.float32)
        tbl_19 = 0.05 * jax.random.normal(jax.random.fold_in(_tk, 500 + 19), (125000, 32), jnp.float32)
        tbl_20 = 0.05 * jax.random.normal(jax.random.fold_in(_tk, 500 + 20), (1250, 32), jnp.float32)
        tbl_21 = 0.05 * jax.random.normal(jax.random.fold_in(_tk, 500 + 21), (1250, 32), jnp.float32)
        tbl_22 = 0.05 * jax.random.normal(jax.random.fold_in(_tk, 500 + 22), (12500, 32), jnp.float32)
        tbl_23 = 0.05 * jax.random.normal(jax.random.fold_in(_tk, 500 + 23), (1250, 32), jnp.float32)
        tbl_24 = 0.05 * jax.random.normal(jax.random.fold_in(_tk, 500 + 24), (1000, 32), jnp.float32)
        tbl_25 = 0.05 * jax.random.normal(jax.random.fold_in(_tk, 500 + 25), (12500, 32), jnp.float32)
        tbl_26 = 0.05 * jax.random.normal(jax.random.fold_in(_tk, 500 + 26), (1000, 32), jnp.float32)
        tbl_27 = 0.05 * jax.random.normal(jax.random.fold_in(_tk, 500 + 27), (12500, 32), jnp.float32)
        tbl_28 = 0.05 * jax.random.normal(jax.random.fold_in(_tk, 500 + 28), (1000, 32), jnp.float32)
        tbl_29 = 0.05 * jax.random.normal(jax.random.fold_in(_tk, 500 + 29), (125000, 32), jnp.float32)
        tbl_30 = 0.05 * jax.random.normal(jax.random.fold_in(_tk, 500 + 30), (1000, 32), jnp.float32)
        tbl_31 = 0.05 * jax.random.normal(jax.random.fold_in(_tk, 500 + 31), (12500, 32), jnp.float32)
        tbl_32 = 0.05 * jax.random.normal(jax.random.fold_in(_tk, 500 + 32), (1250, 32), jnp.float32)
        tbl_33 = 0.05 * jax.random.normal(jax.random.fold_in(_tk, 500 + 33), (1250, 32), jnp.float32)
        tbl_34 = 0.05 * jax.random.normal(jax.random.fold_in(_tk, 500 + 34), (1000, 32), jnp.float32)
        tbl_35 = 0.05 * jax.random.normal(jax.random.fold_in(_tk, 500 + 35), (1250, 32), jnp.float32)
        tbl_36 = 0.05 * jax.random.normal(jax.random.fold_in(_tk, 500 + 36), (12500, 32), jnp.float32)
        tbl_37 = 0.05 * jax.random.normal(jax.random.fold_in(_tk, 500 + 37), (12500, 32), jnp.float32)
        tbl_38 = 0.05 * jax.random.normal(jax.random.fold_in(_tk, 500 + 38), (1000, 32), jnp.float32)
        _rk = jax.random.fold_in(_tk, 7)
        W_top1 = 0.0363456 * jax.random.normal(jax.random.fold_in(_tk, 801), (757, 512), jnp.float32)
        W_top2 = 0.0441942 * jax.random.normal(jax.random.fold_in(_tk, 802), (512, 256), jnp.float32)
        W_top3 = 0.0625 * jax.random.normal(jax.random.fold_in(_tk, 803), (256, 1), jnp.float32)
        b_top1 = jnp.zeros((512,), jnp.float32)
        b_top2 = jnp.zeros((256,), jnp.float32)
        return (dense_ctx, ids, tbl_0, tbl_1, tbl_2, tbl_3, tbl_4, tbl_5, tbl_6, tbl_7, tbl_8, tbl_9, tbl_10, tbl_11, tbl_12, tbl_13, tbl_14, tbl_15, tbl_16, tbl_17, tbl_18, tbl_19, tbl_20, tbl_21, tbl_22, tbl_23, tbl_24, tbl_25, tbl_26, tbl_27, tbl_28, tbl_29, tbl_30, tbl_31, tbl_32, tbl_33, tbl_34, tbl_35, tbl_36, tbl_37, tbl_38, W_top1, b_top1, W_top2, b_top2, W_top3)
    dense_ctx, ids, tbl_0, tbl_1, tbl_2, tbl_3, tbl_4, tbl_5, tbl_6, tbl_7, tbl_8, tbl_9, tbl_10, tbl_11, tbl_12, tbl_13, tbl_14, tbl_15, tbl_16, tbl_17, tbl_18, tbl_19, tbl_20, tbl_21, tbl_22, tbl_23, tbl_24, tbl_25, tbl_26, tbl_27, tbl_28, tbl_29, tbl_30, tbl_31, tbl_32, tbl_33, tbl_34, tbl_35, tbl_36, tbl_37, tbl_38, W_top1, b_top1, W_top2, b_top2, W_top3 = _rec_inputs()

    def _L0_rec_setup():
        import jax, jax.numpy as jnp
        import numpy as np
        F = 39

        def _pair_indices(f):
            row, col = ([], [])
            for i in range(f - 1):
                for j in range(i + 1, f):
                    row.append(i)
                    col.append(j)
            return (np.array(row, np.int32), np.array(col, np.int32))
        ROW, COL = _pair_indices(F)
        key = jax.random.key(seed)
        k1, k2 = jax.random.split(key)
        B, k = (1024, 32)
        P = F * (F - 1) // 2
        inputs = jax.random.normal(k1, (B, F, k), dtype=jnp.float32)
        w = jax.random.normal(k2, (k, P, k), dtype=jnp.float32)
        return {'inputs': inputs, 'w': w}
    _L0_rec_all = _L0_rec_setup()
    _L0_rec_in = {k: v for k, v in _L0_rec_all.items() if k in ('w',)}
    del _L0_rec_all
    return {'dense_ctx': dense_ctx, 'ids': ids, 'tbl_0': tbl_0, 'tbl_1': tbl_1, 'tbl_2': tbl_2, 'tbl_3': tbl_3, 'tbl_4': tbl_4, 'tbl_5': tbl_5, 'tbl_6': tbl_6, 'tbl_7': tbl_7, 'tbl_8': tbl_8, 'tbl_9': tbl_9, 'tbl_10': tbl_10, 'tbl_11': tbl_11, 'tbl_12': tbl_12, 'tbl_13': tbl_13, 'tbl_14': tbl_14, 'tbl_15': tbl_15, 'tbl_16': tbl_16, 'tbl_17': tbl_17, 'tbl_18': tbl_18, 'tbl_19': tbl_19, 'tbl_20': tbl_20, 'tbl_21': tbl_21, 'tbl_22': tbl_22, 'tbl_23': tbl_23, 'tbl_24': tbl_24, 'tbl_25': tbl_25, 'tbl_26': tbl_26, 'tbl_27': tbl_27, 'tbl_28': tbl_28, 'tbl_29': tbl_29, 'tbl_30': tbl_30, 'tbl_31': tbl_31, 'tbl_32': tbl_32, 'tbl_33': tbl_33, 'tbl_34': tbl_34, 'tbl_35': tbl_35, 'tbl_36': tbl_36, 'tbl_37': tbl_37, 'tbl_38': tbl_38, 'W_top1': W_top1, 'b_top1': b_top1, 'W_top2': W_top2, 'b_top2': b_top2, 'W_top3': W_top3, 'L0_rec_w': _L0_rec_in['w']}

def reference(dense_ctx, ids, tbl_0, tbl_1, tbl_2, tbl_3, tbl_4, tbl_5, tbl_6, tbl_7, tbl_8, tbl_9, tbl_10, tbl_11, tbl_12, tbl_13, tbl_14, tbl_15, tbl_16, tbl_17, tbl_18, tbl_19, tbl_20, tbl_21, tbl_22, tbl_23, tbl_24, tbl_25, tbl_26, tbl_27, tbl_28, tbl_29, tbl_30, tbl_31, tbl_32, tbl_33, tbl_34, tbl_35, tbl_36, tbl_37, tbl_38, W_top1, b_top1, W_top2, b_top2, W_top3, L0_rec_w):
    import jax
    import jax.numpy as jnp

    def _L0_rec_ref(inputs, w):
        import jax, jax.numpy as jnp
        import numpy as np
        F = 39

        def _pair_indices(f):
            row, col = ([], [])
            for i in range(f - 1):
                for j in range(i + 1, f):
                    row.append(i)
                    col.append(j)
            return (np.array(row, np.int32), np.array(col, np.int32))
        ROW, COL = _pair_indices(F)
        p = inputs[:, ROW, :]
        q = inputs[:, COL, :]
        return jnp.einsum('bpc,apc,bpa->bp', p, w, q)
    e = jnp.stack([tbl_0[ids[:, 0]], tbl_1[ids[:, 1]], tbl_2[ids[:, 2]], tbl_3[ids[:, 3]], tbl_4[ids[:, 4]], tbl_5[ids[:, 5]], tbl_6[ids[:, 6]], tbl_7[ids[:, 7]], tbl_8[ids[:, 8]], tbl_9[ids[:, 9]], tbl_10[ids[:, 10]], tbl_11[ids[:, 11]], tbl_12[ids[:, 12]], tbl_13[ids[:, 13]], tbl_14[ids[:, 14]], tbl_15[ids[:, 15]], tbl_16[ids[:, 16]], tbl_17[ids[:, 17]], tbl_18[ids[:, 18]], tbl_19[ids[:, 19]], tbl_20[ids[:, 20]], tbl_21[ids[:, 21]], tbl_22[ids[:, 22]], tbl_23[ids[:, 23]], tbl_24[ids[:, 24]], tbl_25[ids[:, 25]], tbl_26[ids[:, 26]], tbl_27[ids[:, 27]], tbl_28[ids[:, 28]], tbl_29[ids[:, 29]], tbl_30[ids[:, 30]], tbl_31[ids[:, 31]], tbl_32[ids[:, 32]], tbl_33[ids[:, 33]], tbl_34[ids[:, 34]], tbl_35[ids[:, 35]], tbl_36[ids[:, 36]], tbl_37[ids[:, 37]], tbl_38[ids[:, 38]]], axis=1)
    z = _L0_rec_ref(e, L0_rec_w)
    z = z.reshape(z.shape[0], -1)
    h = jnp.concatenate([z, dense_ctx], axis=1)
    h = jnp.maximum(h @ W_top1 + b_top1, 0.0)
    h = jnp.maximum(h @ W_top2 + b_top2, 0.0)
    y = h @ W_top3
    return y

_drawn_inputs = setup_inputs


def setup_inputs(seed=0):
    import zlib

    import numpy as np

    out = dict(_drawn_inputs(seed))
    spreads = {'b_top1': (0.0, 0.1), 'b_top2': (0.0, 0.1)}
    factors = {}
    for name, (base, spread) in spreads.items():
        noise = np.random.default_rng([zlib.crc32(name.encode()), seed]).standard_normal(out[name].shape)
        drawn = base * np.exp(spread * noise) if base else spread * noise
        out[name] = jnp.asarray(drawn.astype(out[name].dtype))
    for name, factor in factors.items():
        out[name] = (out[name] * factor).astype(out[name].dtype)
    return out
```

```python
import concourse.bass as bass
from concourse import mybir
from contextlib import ExitStack

F = 39
D = 32
B = 512
P = 128
BT = B // P
Q = P // D
NBLK = (F + Q - 1) // Q
NPAIR = F * (F - 1) // 2
DENSE = 16
H1, H2 = 512, 256


def pair_index(i, j):
    return i * F - i * (i + 1) // 2 + (j - i - 1)


def plan():
    chunks = []
    for f in range(F):
        n = f // Q
        cross = [(m, [(f, tuple(range(Q)))]) for m in range(n)]
        for m in range(0, n - 1, 2):
            chunks.append((f, cross[m:m + 2]))
        if n % 2:
            if f % 2:
                chunks.append((f, [(n - 1, [(f - 1, tuple(range(Q)))]), cross[n - 1]]))
            elif f == F - 1:
                chunks.append((f, [cross[n - 1], (n, [(Q * n + 1, (0,)), (Q * n + 2, (1,)), (Q * n, (2,))])]))
        if f % Q == Q - 1:
            a = Q * n
            chunks.append((f, [(n, [(a + 1, (0, 2, 3))]), (n, [(a + 2, (0,)), (a, (3,)), (a + 3, (2,))])]))
    return chunks


CHUNKS = plan()
TILES = [t for _, tiles in CHUNKS for t in tiles]
PARTS = [(m, f, qs) for m, parts in TILES for f, qs in parts]
NT, NW = len(TILES), len(PARTS)
FIRST_TILE = [sum(len(t) for _, t in CHUNKS[:k]) for k in range(len(CHUNKS) + 1)]
FIRST_PART = [sum(len(p) for _, t in CHUNKS[:k] for _, p in t) for k in range(len(CHUNKS) + 1)]
PIECE = 16
NPIECE = (NW + PIECE - 1) // PIECE
WC = PIECE * P // Q
ROWS_T = P // Q
KT = (NT + ROWS_T - 1) // ROWS_T
NBATCH = (NT + Q - 1) // Q
TBUF, PRODS, WRING, EHL, NAT = 3, 5, 3, 3, 3
FLUSH = (3, 5)


def z_row(t, q):
    return t // ROWS_T, D * (t % Q) + Q * ((t % ROWS_T) // Q) + q


def batch_of(t):
    return t // Q


def last_chunk_of(batch):
    last = min(Q * batch + Q, NT) - 1
    return next(k for k in range(len(CHUNKS)) if FIRST_TILE[k + 1] > last)


def steps():
    out = [("weights", i) for i in range(3)]
    piece = 3
    layer1 = [(done, (use, m)) for use, done in enumerate(FLUSH) for m in range(H1 // P)]
    next_layer1 = 0
    first_use = [next((k for k, c in enumerate(CHUNKS) if any(g == f for _, p in c[1] for g, _ in p)), len(CHUNKS))
                 for f in range(F)]
    need = [min(first_use[f:]) for f in range(F)]
    split, stack = 0, 0

    def stacked():
        nonlocal stack
        out.append(("feature", stack))
        stack += 1
        if stack % Q == 0 or stack == F:
            out.append(("block", (stack - 1) // Q))

    for k in range(len(CHUNKS)):
        while split < F and need[split] <= k + AHEAD_SPLIT:
            if split - stack >= EHL - 1:
                stacked()
            out.append(("split", split))
            split += 1
        while stack < F and need[stack] <= k + AHEAD_STACK:
            stacked()
        while piece < NPIECE and FIRST_PART[k] >= PIECE * (piece - 3) + 4:
            out.append(("weights", piece))
            piece += 1
        out.append(("chunk", k))
        if layer1 and k >= max(last_chunk_of(layer1[0][0] * ROWS_T // Q - 1) + 5, next_layer1):
            out.append(("layer1", *layer1.pop(0)[1]))
            next_layer1 = k + 3
    for _, unit in layer1:
        out.append(("layer1", *unit))
    return out


AHEAD_SPLIT, AHEAD_STACK = 5, 2
STEPS = steps()
SPARE = [s for s in STEPS if s[0] in ("feature", "block", "layer1")]
USE = {s: n for n, s in enumerate(SPARE)}


def tower(nc, dense_t, ids_t, tables, w_dense, w1_z, w1_dense, b1_t, w2_t, b2_t, w3_t, ident_c, select_c, out):
    fp32 = mybir.dt.float32
    fp32r = mybir.dt.float32r
    ALU = mybir.AluOpType
    ACT = mybir.ActivationFunctionType
    w_split = nc.dram_tensor("w_split", (NPIECE, 2, P, WC), fp32, kind="Internal").ap()

    ctx = ExitStack()
    with ctx:
        def sb(name, shape, dt=fp32):
            return ctx.enter_context(nc.sbuf_tensor(name, shape, dt))

        def sem(name):
            return ctx.enter_context(nc.semaphore(name))

        ids = sb("ids_sb", [P, F * BT], mybir.dt.int32)
        e_nat = sb("e_nat", [P, NAT, BT, Q, D])
        e_parts = sb("e_parts", [P, EHL, BT, 2, 2, D])
        e_stack = sb("e_stack", [P, F, B], fp32r)
        e_blk = sb("e_blk", [P, NBLK, B])
        w_raw = sb("w_raw", [P, 2, WC])
        w_parts = sb("w_parts", [P, 2, 2, WC], fp32r)
        w_ring = sb("w_ring", [P, WRING, PIECE, P], fp32r)
        prod = sb("prod", [P, PRODS, 2, B])
        z = sb("z", [P, KT, B])
        w1 = sb("w1", [P, KT, H1])
        w1d = sb("w1d", [DENSE, H1])
        dense = sb("dense", [DENSE, B])
        w2 = sb("w2", [P, H1 // P, H2])
        w3 = sb("w3", [P, H2 // P])
        b1 = sb("b1", [P, H1 // P])
        b2 = sb("b2", [P, H2 // P])
        h1 = sb("h1", [P, H1 // P, B])
        h2 = prod[:, 0]
        y = prod[0:1, 1, 0, :]
        ident = sb("ident", [P, P])
        select = sb("select", [P, 2 * D - Q])

        t_ps = [ctx.enter_context(nc.psum_tensor(f"t_ps{i}", [P, 2, B], fp32)) for i in range(TBUF)]
        z_ps = ctx.enter_context(nc.psum_tensor("z_ps", [P, B], fp32))
        spare = ctx.enter_context(nc.psum_tensor("spare", [P, B], fp32))
        h1_ps = [t_ps[m // 2][:, m % 2, :] for m in range(H1 // P)]
        h2_ps = [t_ps[2][:, m, :] for m in range(H2 // P)]
        y_ps = z_ps[0:1, :]

        ids_in = sem("ids_in")
        consts_in = sem("consts_in")
        top_in = sem("top_in")
        gathered = [sem(f"gathered{f}") for f in range(F)]
        pad_zeroed = sem("pad_zeroed")
        e_high = sem("e_high")
        e_low = sem("e_low")
        spare_filled = sem("spare_filled")
        spare_out = sem("spare_out")
        w_raw_in = [sem(f"w_raw_in{i}") for i in range(2)]
        w_high = sem("w_high")
        w_low = sem("w_low")
        w_saved = sem("w_saved")
        w_loaded = [sem(f"w_loaded{i}") for i in range(WRING)]
        t_ready = sem("t_ready")
        prod_ready = sem("prod_ready")
        summed = sem("summed")
        z_out = sem("z_out")
        h1_sum = sem("h1_sum")
        h1_added = sem("h1_added")
        h1_ready = sem("h1_ready")
        h2_sum = sem("h2_sum")
        h2_ready = sem("h2_ready")
        y_sum = sem("y_sum")
        y_ready = sem("y_ready")
        y_stored = sem("y_stored")

        def rows_twice(f):
            rows = e_nat[:, f // Q % NAT, :, f % Q, :]
            return bass.AP(rows.tensor, rows.offset, [rows.ap[0], rows.ap[1], [0, 2], rows.ap[2]])

        block = ctx.enter_context(nc.Block())

        @block.gpsimd
        def _(pool):
            nc.gpsimd.memset(e_blk[P - D:P, NBLK - 1, :], 0.0).then_inc(pad_zeroed, 1)
            pool.wait_ge(ids_in, 16)
            for f in range(F):
                if f % Q == 0 and f // Q >= NAT:
                    pool.wait_ge(spare_filled, USE["block", f // Q - NAT] + 1)
                for bt in range(BT):
                    at = f * BT + bt
                    pool.indirect_dma_start(
                        out=e_nat[:, f // Q % NAT, bt, f % Q, :], out_offset=None, in_=tables[f],
                        in_offset=bass.IndirectOffsetOnAxis(ap=ids[:, at:at + 1], axis=0),
                    ).then_inc(gathered[f], 16)

        @block.sync
        def _(sp):
            def raw(i):
                if i >= 2:
                    sp.wait_ge(w_high, i - 1)
                    sp.wait_ge(w_low, i - 1)
                sp.dma_start(w_raw[:, i % 2, :], w_dense[i]).then_inc(w_raw_in[i % 2], 16)

            sp.dma_start(ids[:], ids_t).then_inc(ids_in, 16)
            raw(0)
            sp.dma_start(ident[:], ident_c).then_inc(consts_in, 16)
            sp.dma_start(select[:], select_c).then_inc(consts_in, 16)
            raw(1)
            for i in range(NPIECE):
                sp.wait_ge(w_high, i + 1)
                sp.wait_ge(w_low, i + 1)
                sp.dma_start(w_split[i].rearrange("s p x -> p s x"),
                             w_parts[:, i % 2].bitcast(fp32)).then_inc(w_saved, 16)
                if i + 2 < NPIECE:
                    raw(i + 2)
                sp.wait_ge(w_saved, 16 * (i + 1))
                if i >= WRING:
                    last = PIECE * (i - WRING + 1)
                    sp.wait_ge(t_ready, next(k for k in range(len(CHUNKS)) if FIRST_PART[k + 1] >= last) + 1)
                for s in range(2):
                    piece = w_split[i, s]
                    twice = bass.AP(piece.tensor, piece.offset, [[0, 2], [Q * WC, D], [1, Q * WC]])
                    sp.dma_start(w_ring[2 * D * s:2 * D * (s + 1), i % WRING].bitcast(fp32).rearrange("p a b -> p (a b)"),
                                 twice).then_inc(w_loaded[i % WRING], 16)
                if i == 2:
                    sp.dma_start(w1[:], w1_z).then_inc(top_in, 16)
                    sp.dma_start(w1d[:], w1_dense).then_inc(top_in, 16)
                    sp.dma_start(dense[:], dense_t).then_inc(top_in, 16)
                    sp.dma_start(w2[:], w2_t).then_inc(top_in, 16)
                    sp.dma_start(w3[:], w3_t).then_inc(top_in, 16)
                    sp.dma_start(b1[:], b1_t).then_inc(top_in, 16)
                    sp.dma_start(b2[:], b2_t).then_inc(top_in, 16)
            sp.wait_ge(y_ready, 1)
            sp.dma_start(out.rearrange("b o -> o b"), y).then_inc(y_stored, 16)
            sp.wait_ge(y_stored, 16)

        @block.scalar
        def _(act):
            z_taken = 0
            top_waited = False

            def take_z():
                nonlocal z_taken
                last = min(ROWS_T // Q * (z_taken + 1), NBATCH)
                act.wait_ge(summed, last)
                nc.scalar.copy(z[:, z_taken, :], z_ps[:]).then_inc(z_out, 1)
                z_taken += 1

            for step in STEPS:
                if step[0] == "weights":
                    i = step[1]
                    act.wait_ge(w_raw_in[i % 2], 16 * (i // 2 + 1))
                    if i >= 2:
                        act.wait_ge(w_saved, 16 * (i - 1))
                    nc.scalar.copy(w_parts[:, i % 2, 0, :], w_raw[:, i % 2, :]).then_inc(w_high, 1)
                elif step[0] == "split":
                    f = step[1]
                    act.wait_ge(gathered[f], 16 * BT)
                    if f >= EHL:
                        act.wait_ge(spare_filled, USE["feature", f - EHL] + 1)
                    nc.scalar.copy(e_parts[:, f % EHL, :, :, 0, :].bitcast(fp32r), rows_twice(f)).then_inc(e_high, 1)
                elif step[0] == "feature":
                    f = step[1]
                    act.wait_ge(spare_filled, USE[step] + 1)
                    nc.scalar.copy(e_stack[:, f, :], spare[:]).then_inc(spare_out, 1)
                elif step[0] == "block":
                    n = step[1]
                    rows = min(F - Q * n, Q) * D
                    act.wait_ge(spare_filled, USE[step] + 1)
                    nc.scalar.copy(e_blk[0:rows, n, :], spare[0:rows, :]).then_inc(spare_out, 1)
                elif step[0] == "layer1" and step[1] == 0:
                    m = step[2]
                    if not top_waited:
                        act.wait_ge(top_in, 16 * 7)
                        top_waited = True
                    act.wait_ge(spare_filled, USE[step] + 1)
                    nc.scalar.activation(h1[:, m, :], spare[:], ACT.Identity, bias=b1[:, m:m + 1]).then_inc(spare_out, 1)
                elif step[0] == "chunk":
                    if z_taken < KT - 1 and step[1] >= last_chunk_of(ROWS_T // Q * (z_taken + 1) - 1) + 3:
                        take_z()
            while z_taken < KT:
                take_z()
            for m in range(H1 // P):
                act.wait_ge(h1_added, m + 1)
                nc.scalar.activation(h1[:, m, :], h1[:, m, :], ACT.Relu).then_inc(h1_ready, 1)
            for m in range(H2 // P):
                act.wait_ge(h2_sum, m + 1)
                nc.scalar.activation(h2[:, m, :], h2_ps[m], ACT.Relu, bias=b2[:, m:m + 1]).then_inc(h2_ready, 1)
            act.wait_ge(y_sum, 1)
            nc.scalar.copy(y, y_ps).then_inc(y_ready, 1)

        @block.vector
        def _(dve):
            dve.wait_ge(pad_zeroed, 1)
            for step in STEPS:
                if step[0] == "weights":
                    i = step[1]
                    dve.wait_ge(w_high, i + 1)
                    nc.vector.tensor_tensor(w_parts[:, i % 2, 1, :], w_raw[:, i % 2, :],
                                            w_parts[:, i % 2, 0, :].bitcast(fp32), ALU.subtract).then_inc(w_low, 1)
                elif step[0] == "split":
                    f = step[1]
                    dve.wait_ge(e_high, f + 1)
                    nc.vector.tensor_tensor(e_parts[:, f % EHL, :, :, 1, :].bitcast(fp32r), rows_twice(f),
                                            e_parts[:, f % EHL, :, :, 0, :], ALU.subtract).then_inc(e_low, 1)
                elif step[0] == "chunk":
                    k = step[1]
                    tiles = CHUNKS[k][1]
                    first, n = tiles[0][0], len(tiles)
                    by = e_blk[:, first:first + 2, :]
                    if tiles[-1][0] == first:
                        by = e_blk[:, first:first + 1, :].to_broadcast([P, n, B])
                    dve.wait_ge(t_ready, k + 1)
                    dve.wait_ge(spare_out, USE["block", tiles[-1][0]] + 1)
                    if k >= PRODS:
                        dve.wait_ge(summed, batch_of(FIRST_TILE[k - PRODS + 1] - 1) + 1)
                    nc.vector.tensor_tensor(prod[:, k % PRODS, 0:n, :], t_ps[k % TBUF][:, 0:n, :], by,
                                            ALU.mult).then_inc(prod_ready, 1)
                elif step[0] == "layer1" and step[1] == 1:
                    m = step[2]
                    dve.wait_ge(spare_filled, USE[step] + 1)
                    nc.vector.tensor_tensor(h1[:, m, :], spare[:], h1[:, m, :], ALU.add).then_inc(spare_out, 1)
            for m in range(H1 // P):
                dve.wait_ge(h1_sum, m + 1)
                nc.vector.tensor_tensor(h1[:, m, :], h1_ps[m], h1[:, m, :], ALU.add).then_inc(h1_added, 1)

        @block.tensor
        def _(pe):
            batches = 0

            def sums(upto):
                nonlocal batches
                while batches < NBATCH and last_chunk_of(batches) < upto:
                    b = batches
                    pe.wait_ge(prod_ready, last_chunk_of(b) + 1)
                    per = ROWS_T // Q
                    if b % per == 0 and b:
                        pe.wait_ge(z_out, b // per)
                    for t in range(Q * b, min(Q * b + Q, NT)):
                        k = next(k for k in range(len(CHUNKS)) if FIRST_TILE[k + 1] > t)
                        g, at = t % Q, Q * (b % per)
                        last = nc.tensor.matmul(z_ps[D * g:D * (g + 1), :], select[:, D - Q - at:2 * D - Q - at],
                                                prod[:, k % PRODS, t - FIRST_TILE[k], :],
                                                start=(b % per == 0), stop=(b % per == per - 1 or t + Q >= NT))
                    last.then_inc(summed, 1)
                    batches += 1

            def spare_free(step):
                if USE[step]:
                    pe.wait_ge(spare_out, USE[step])

            stacks = 0
            pe.wait_ge(consts_in, 32)
            top_waited = False
            for step in STEPS:
                if step[0] == "feature":
                    f = step[1]
                    pe.wait_ge(e_high, f + 1)
                    pe.wait_ge(e_low, f + 1)
                    spare_free(step)
                    for bt in range(BT):
                        parts = e_parts[:, f % EHL, bt].rearrange("p r s x -> p (r s x)")
                        last = nc.tensor.transpose(spare[:, bt * P:(bt + 1) * P], parts, ident[:])
                    last.then_inc(spare_filled, 1)
                elif step[0] == "block":
                    n = step[1]
                    fs = min(F - Q * n, Q)
                    spare_free(step)
                    for bt in range(BT):
                        last = nc.tensor.transpose(spare[0:fs * D, bt * P:(bt + 1) * P],
                                                   e_nat[:, n % NAT, bt, 0:fs, :].rearrange("p f x -> p (f x)"), ident[:])
                    last.then_inc(spare_filled, 1)
                elif step[0] == "layer1":
                    use, m = step[1:]
                    cols = slice(m * P, (m + 1) * P)
                    if not top_waited:
                        pe.wait_ge(top_in, 16 * 7)
                        top_waited = True
                    spare_free(step)
                    pe.wait_ge(z_out, FLUSH[use])
                    kts = range(FLUSH[use - 1] if use else 0, FLUSH[use])
                    if use == 0:
                        nc.tensor.matmul(spare[:], w1d[:, cols], dense[:], start=True, stop=False)
                    for kt in kts:
                        last = nc.tensor.matmul(spare[:], w1[:, kt, cols], z[:, kt, :],
                                                start=(use > 0 and kt == kts[0]), stop=(kt == kts[-1]))
                    last.then_inc(spare_filled, 1)
                elif step[0] == "chunk":
                    k = step[1]
                    sums(k - TBUF + 1)
                    if k >= TBUF:
                        pe.wait_ge(prod_ready, k - TBUF + 1)
                    part = FIRST_PART[k]
                    for n, (m, parts) in enumerate(CHUNKS[k][1]):
                        for at, (f, qs) in enumerate(parts):
                            i = part // PIECE
                            if part % PIECE == 0:
                                pe.wait_ge(w_loaded[i % WRING], 32 * (i // WRING + 1))
                            if USE["feature", f] + 1 > stacks:
                                stacks = USE["feature", f] + 1
                                pe.wait_ge(spare_out, stacks)
                            last = nc.tensor.matmul(t_ps[k % TBUF][:, n, :], w_ring[:, i % WRING, part % PIECE, :],
                                                    e_stack[:, f, :], start=(at == 0), stop=(at == len(parts) - 1))
                            part += 1
                    last.then_inc(t_ready, 1)
            sums(len(CHUNKS))

            pe.wait_ge(z_out, KT)
            for m in range(H1 // P):
                for kt in range(FLUSH[-1], KT):
                    last = nc.tensor.matmul(h1_ps[m], w1[:, kt, m * P:(m + 1) * P], z[:, kt, :],
                                            start=(kt == FLUSH[-1]), stop=(kt == KT - 1))
                last.then_inc(h1_sum, 1)
            for kt in range(H1 // P):
                pe.wait_ge(h1_ready, kt + 1)
                for m in range(H2 // P):
                    last = nc.tensor.matmul(h2_ps[m], w2[:, kt, m * P:(m + 1) * P], h1[:, kt, :],
                                            start=(kt == 0), stop=(kt == H1 // P - 1))
                    if kt == H1 // P - 1:
                        last.then_inc(h2_sum, 1)
            for m in range(H2 // P):
                pe.wait_ge(h2_ready, m + 1)
                last = nc.tensor.matmul(y_ps, w3[:, m:m + 1], h2[:, m, :], start=(m == 0), stop=(m == H2 // P - 1))
            last.then_inc(y_sum, 1)


def lay_out(inputs):
    import numpy as np

    def array(name):
        return np.ascontiguousarray(inputs[name])

    arrays = {f"tbl_{f}": array(f"tbl_{f}") for f in range(F)}
    arrays["ids"] = np.ascontiguousarray(array("ids").reshape(BT, P, F).transpose(1, 2, 0).reshape(P, F * BT))
    arrays["dense"] = np.ascontiguousarray(array("dense_ctx").T)
    w = array("L0_rec_w")
    parts = np.zeros((D, NPIECE * PIECE, Q, D), w.dtype)
    for n, (m, f, qs) in enumerate(PARTS):
        for q in qs:
            g = Q * m + q
            parts[:, n, q, :] = w[:, pair_index(g, f), :] if g < f else w[:, pair_index(f, g), :].T
    arrays["w"] = np.ascontiguousarray(parts.reshape(D, NPIECE, Q * WC).transpose(1, 0, 2).reshape(NPIECE, P, WC))
    w1 = array("W_top1")
    w1_z = np.zeros((P, KT, H1), w1.dtype)
    for t, (m, parts_) in enumerate(TILES):
        kt = z_row(t, 0)[0]
        for f, qs in parts_:
            for q in qs:
                g = Q * m + q
                w1_z[z_row(t, q)[1], kt] = w1[pair_index(min(f, g), max(f, g))]
    arrays["w1_z"] = w1_z
    arrays["w1_dense"] = np.ascontiguousarray(w1[NPAIR:])
    arrays["b1"] = np.ascontiguousarray(array("b_top1").reshape(H1 // P, P).T)
    arrays["w2"] = np.ascontiguousarray(array("W_top2").reshape(H1 // P, P, H2).transpose(1, 0, 2))
    arrays["b2"] = np.ascontiguousarray(array("b_top2").reshape(H2 // P, P).T)
    arrays["w3"] = np.ascontiguousarray(array("W_top3").reshape(H2 // P, P).T)
    arrays["ident"] = np.eye(P, dtype=np.float32)
    select = np.zeros((P, 2 * D - Q), np.float32)
    for q in range(Q):
        select[D * q:D * (q + 1), D - Q + q] = 1.0
    arrays["select"] = select
    return arrays


def kernel(**inputs):
    import concourse.bacc as _bacc
    from concourse import mybir as _mybir
    from concourse.bass_utils import run_bass_kernel_spmd as _run

    nc = _bacc.Bacc("TRN2", target_bir_lowering=False, num_devices=1)
    arrays = {f"in_{name}": a for name, a in lay_out(inputs).items()}
    aps = {name: nc.dram_tensor(name, a.shape, _mybir.dt.from_np(a.dtype), kind="ExternalInput").ap()
           for name, a in arrays.items()}
    out = nc.dram_tensor("out_y", (B, 1), _mybir.dt.float32, kind="ExternalOutput").ap()
    tower(nc, aps["in_dense"], aps["in_ids"], [aps[f"in_tbl_{f}"] for f in range(F)], aps["in_w"], aps["in_w1_z"],
          aps["in_w1_dense"], aps["in_b1"], aps["in_w2"], aps["in_b2"], aps["in_w3"], aps["in_ident"],
          aps["in_select"], out)
    r = _run(nc, [arrays], core_ids=[0])
    return r.results[0]["out_y"]
```

```python
import concourse.bass as bass
from concourse import mybir
from contextlib import ExitStack

F = 39
D = 32
B = 512
P = 128
BT = B // P
Q = P // D
NBLK = (F + Q - 1) // Q
ROWS = [125000, 1000, 1250, 1000, 1250, 1250, 12500, 1250, 1250, 125000, 1250, 12500, 1250, 12500, 12500, 125000, 1250,
        1000, 125000, 125000, 1250, 1250, 12500, 1250, 1000, 12500, 1000, 12500, 1000, 125000, 1000, 12500, 1250, 1250,
        1000, 1250, 12500, 12500, 1000]
KH = 125
NHOT = 2
HOT = sorted(range(F), key=lambda f: ROWS[f])[:Q * NHOT]
ORDER = HOT + [f for f in range(F) if f not in HOT]
J = [max(ROWS[ORDER[Q * n + q]] for q in range(Q)) // KH for n in range(NHOT)]
JMAX = max(J)
NPAIR = F * (F - 1) // 2
DENSE = 16
H1, H2 = 512, 256


def pair_index(i, j):
    return i * F - i * (i + 1) // 2 + (j - i - 1)


def plan():
    chunks = []
    for f in range(F):
        n = f // Q
        cross = [(m, [(f, tuple(range(Q)))]) for m in range(n)]
        for m in range(0, n - 1, 2):
            chunks.append((f, cross[m:m + 2]))
        if n % 2:
            if f % 2:
                chunks.append((f, [(n - 1, [(f - 1, tuple(range(Q)))]), cross[n - 1]]))
            elif f == F - 1:
                chunks.append((f, [cross[n - 1], (n, [(Q * n + 1, (0,)), (Q * n + 2, (1,)), (Q * n, (2,))])]))
        if f % Q == Q - 1:
            a = Q * n
            chunks.append((f, [(n, [(a + 1, (0, 2, 3))]), (n, [(a + 2, (0,)), (a, (3,)), (a + 3, (2,))])]))
    return chunks


CHUNKS = plan()
TILES = [t for _, tiles in CHUNKS for t in tiles]
PARTS = [(m, f, qs) for m, parts in TILES for f, qs in parts]
NT, NW = len(TILES), len(PARTS)
FIRST_TILE = [sum(len(t) for _, t in CHUNKS[:k]) for k in range(len(CHUNKS) + 1)]
FIRST_PART = [sum(len(p) for _, t in CHUNKS[:k] for _, p in t) for k in range(len(CHUNKS) + 1)]
PIECE = 16
NPIECE = (NW + PIECE - 1) // PIECE
WC = PIECE * P // Q
ROWS_T = P // Q
KT = (NT + ROWS_T - 1) // ROWS_T
NBATCH = (NT + Q - 1) // Q
TBUF, WRING, EHL, NAT = 3, 3, 3, 3
PRODS = 5
FLUSH = (2, 4, 5)


def z_row(t, q):
    return t // ROWS_T, D * (t % Q) + Q * ((t % ROWS_T) // Q) + q


def batch_of(t):
    return t // Q


def last_chunk_of(batch):
    last = min(Q * batch + Q, NT) - 1
    return next(k for k in range(len(CHUNKS)) if FIRST_TILE[k + 1] > last)


def steps():
    out = [("table", 0)]
    piece = 0
    for n in range(NHOT):
        stacks = [("feature", Q * (n - 1) + q) for q in range(Q)] if n else []
        for j in range(J[n]):
            if stacks and j % 2 == 0:
                out.append(stacks.pop(0))
            out.append(("slice", n, j))
            if n + 1 < NHOT and j == 3:
                out.append(("table", n + 1))
            if j % W_SLICES == W_SLICES - 1:
                out.append(("weights", piece))
                piece += 1
        out += stacks + [("picked", n)]
    layer1 = [(done, (use, m)) for use, done in enumerate(FLUSH) for m in range(H1 // P)]
    next_layer1 = 0
    first_use = [next((k for k, c in enumerate(CHUNKS) if any(g == f for _, p in c[1] for g, _ in p)), len(CHUNKS))
                 for f in range(F)]
    need = [min(first_use[f:]) for f in range(F)]
    split, stack = Q * NHOT, Q * (NHOT - 1)

    def stacked():
        nonlocal stack
        out.append(("feature", stack))
        stack += 1
        if stack > Q * NHOT and (stack % Q == 0 or stack == F):
            out.append(("block", (stack - 1) // Q))

    for k in range(len(CHUNKS)):
        while split < F and need[split] <= k + AHEAD_SPLIT:
            if split - stack >= EHL - 1:
                stacked()
            else:
                out.append(("split", split))
                split += 1
        while stack < F and need[stack] <= k + AHEAD_STACK:
            stacked()
        if piece < NPIECE and k % W_CHUNKS == 0:
            out.append(("weights", piece))
            piece += 1
        out.append(("chunk", k))
        if layer1 and k >= max(last_chunk_of(layer1[0][0] * ROWS_T // Q - 1) + 5, next_layer1):
            out.append(("layer1", *layer1.pop(0)[1]))
            next_layer1 = k + LAYER1_GAP
    for _, unit in layer1:
        out.append(("layer1", *unit))
    return out


LAYER1_GAP = 3
W_SLICES = 4
TOP_AT = 30
W_CHUNKS = 2
WBUF = 2
AHEAD_SPLIT = 7
AHEAD_STACK = 3
STEPS = steps()
SPARE = [s for s in STEPS if s[0] in ("feature", "block", "layer1")]
USE = {s: n for n, s in enumerate(SPARE)}


def tower(nc, dense_t, ids_t, tables, hot_ids, hot_rows, pick_c, w_dense, w1_z, w1_dense, b1_t, w2_t, b2_t, w3_t, ident_c, select_c, out):
    fp32 = mybir.dt.float32
    fp32r = mybir.dt.float32r
    bf16 = mybir.dt.bfloat16
    fp16 = mybir.dt.float16
    int32 = mybir.dt.int32
    ALU = mybir.AluOpType
    ACT = mybir.ActivationFunctionType
    w_split = nc.dram_tensor("w_split", (NPIECE, 2, P, WC), fp32, kind="Internal").ap()

    ctx = ExitStack()
    with ctx:
        def sb(name, shape, dt=fp32):
            return ctx.enter_context(nc.sbuf_tensor(name, shape, dt))

        def sem(name):
            return ctx.enter_context(nc.semaphore(name))

        ids = sb("ids_sb", [P, (F - Q * NHOT) * BT], mybir.dt.int32)
        e_nat = sb("e_nat", [P, NAT, BT, Q, D])
        e_parts = sb("e_parts", [P, EHL, BT, 2, 2, D], fp32r)
        e_stack_hot = sb("e_stack_hot", [P, Q * NHOT, B], fp32r)
        e_blk = sb("e_blk", [P, NBLK, B])
        w_raw = sb("w_raw", [P, WBUF, WC])
        w_parts = sb("w_parts", [P, WBUF, 2, WC], fp32r)
        w_ring = sb("w_ring", [P, WRING, PIECE, P], fp32r)
        prod = sb("prod", [P, PRODS, 2, B])
        z = sb("z", [P, KT, B])
        w1 = sb("w1", [P, KT, H1])
        w1d = sb("w1d", [DENSE, H1])
        dense = sb("dense", [DENSE, B])
        w2 = sb("w2", [P, H1 // P, H2])
        w3 = sb("w3", [P, H2 // P])
        b1 = sb("b1", [P, H1 // P])
        b2 = sb("b2", [P, H2 // P])
        h1 = sb("h1", [P, H1 // P, B])
        h2 = prod[:, 0]
        y = prod[0:1, 1, 0, :]
        ident = sb("ident", [P, P])
        select = sb("select", [P, 2 * D - Q])
        ident_r = sb("ident_r", [P, P], fp32r)
        with ExitStack() as early:
            def early_sb(name, shape, dt):
                return early.enter_context(nc.sbuf_tensor(name, shape, dt))

            table = early_sb("table", [KH, NHOT, Q, JMAX, D], fp32)
            table_parts = early_sb("table_parts", [KH, 2, 3, Q, JMAX, D], bf16)
            hot_ids_16 = early_sb("hot_ids_16", [KH, 2, Q * B], fp16)
            row_of = early_sb("row_of", [KH, NHOT * JMAX], fp32)
            pick_in = early_sb("pick_in", [P, 2, P], fp32)
            pick = early_sb("pick", [P, 2, P], fp32r)
            e_high_t = early_sb("e_high_t", [P, B], fp32r)
            e_low_t = early_sb("e_low_t", [P, B], fp32r)
        e_stack_late = sb("e_stack_late", [P, F - Q * NHOT, B], fp32r)
        hot_ids_in = [a[0:KH, 0:Q, :].rearrange("p a b -> p (a b)").bitcast(int32) for a in (h1, w1)]
        onehot = z[0:KH].rearrange("p a b -> p (a b)").bitcast(bf16).rearrange("p (a b) -> p a b", a=KT // 2)

        def e_stack(f):
            return e_stack_hot[:, f, :] if f < Q * NHOT else e_stack_late[:, f - Q * NHOT, :]

        t_ps = [ctx.enter_context(nc.psum_tensor(f"t_ps{i}", [P, 2, B], fp32)) for i in range(TBUF)]
        z_ps = ctx.enter_context(nc.psum_tensor("z_ps", [P, B], fp32))
        spare = ctx.enter_context(nc.psum_tensor("spare", [P, B], fp32))
        h1_ps = [t_ps[m // 2][:, m % 2, :] for m in range(H1 // P)]
        h2_ps = [t_ps[2][:, m, :] for m in range(H2 // P)]
        y_ps = z_ps[0:1, :]

        ids_in = sem("ids_in")
        row_of_in = sem("row_of_in")
        consts_in = sem("consts_in")
        top_in = sem("top_in")
        table_in = [sem(f"table_in{n}") for n in range(NHOT)]
        hot_ids_arrived = [sem(f"hot_ids_arrived{n}") for n in range(2)]
        pick_ready = sem("pick_ready")
        table_high = sem("table_high")
        table_rest = sem("table_rest")
        table_mid = sem("table_mid")
        table_low = sem("table_low")
        hot_ids_ready = sem("hot_ids_ready")
        onehot_ready = sem("onehot_ready")
        onehot_used = sem("onehot_used")
        picked_out = sem("picked_out")
        hot_high = sem("hot_high")
        hot_low = sem("hot_low")
        gathered = [sem(f"gathered{f}") for f in range(F)]
        pad_zeroed = sem("pad_zeroed")
        e_high = sem("e_high")
        e_low = sem("e_low")
        spare_filled = sem("spare_filled")
        spare_out = sem("spare_out")
        w_raw_in = [sem(f"w_raw_in{i}") for i in range(WBUF)]
        w_high = sem("w_high")
        w_low = sem("w_low")
        w_saved = [sem(f"w_saved{i}") for i in range(WBUF)]
        w_loaded = [sem(f"w_loaded{i}") for i in range(WRING)]
        t_ready = sem("t_ready")
        prod_ready = sem("prod_ready")
        summed = sem("summed")
        z_out = sem("z_out")
        h1_sum = sem("h1_sum")
        h1_added = sem("h1_added")
        h1_ready = sem("h1_ready")
        h2_sum = sem("h2_sum")
        h2_ready = sem("h2_ready")
        y_sum = sem("y_sum")
        y_ready = sem("y_ready")
        y_stored = sem("y_stored")

        def rows_twice(f):
            rows = e_nat[:, f // Q % NAT, :, f % Q, :]
            return bass.AP(rows.tensor, rows.offset, [rows.ap[0], rows.ap[1], [0, 2], rows.ap[2]])

        block = ctx.enter_context(nc.Block())

        @block.gpsimd
        def _(pool):
            nc.gpsimd.memset(e_blk[P - D:P, NBLK - 1, :], 0.0).then_inc(pad_zeroed, 1)
            pool.wait_ge(ids_in, 16)

            def gather(f):
                if f % Q == 0 and f // Q >= NAT + NHOT:
                    pool.wait_ge(spare_filled, USE["block", f // Q - NAT] + 1)
                for bt in range(BT):
                    at = (f - Q * NHOT) * BT + bt
                    pool.indirect_dma_start(
                        out=e_nat[:, f // Q % NAT, bt, f % Q, :], out_offset=None, in_=tables[ORDER[f]],
                        in_offset=bass.IndirectOffsetOnAxis(ap=ids[:, at:at + 1], axis=0),
                    ).then_inc(gathered[f], 16)

            for f in range(Q * NHOT, F):
                gather(f)

        @block.sync
        def _(sp):
            def raw(i):
                sp.dma_start(w_raw[:, i % WBUF, :], w_dense[i]).then_inc(w_raw_in[i % WBUF], 16)

            def load(i):
                sp.wait_ge(w_saved[i % WBUF], 16 * (i // WBUF + 1))
                if i >= WRING:
                    last = PIECE * (i - WRING + 1)
                    sp.wait_ge(t_ready, next(k for k in range(len(CHUNKS)) if FIRST_PART[k + 1] >= last) + 1)
                for s in range(2):
                    piece = w_split[i, s]
                    twice = bass.AP(piece.tensor, piece.offset, [[0, 2], [Q * WC, D], [1, Q * WC]])
                    sp.dma_start(w_ring[2 * D * s:2 * D * (s + 1), i % WRING].bitcast(fp32).rearrange("p a b -> p (a b)"),
                                 twice).then_inc(w_loaded[i % WRING], 16)

            def hot(n):
                for q in range(Q):
                    rows = tables[ORDER[Q * n + q]].rearrange("(p j) x -> p j x", p=KH)
                    sp.dma_start(table[:, n, q, 0:rows.shape[1], :], rows).then_inc(table_in[n], 16)
                every = hot_ids[n]
                every = bass.AP(every.tensor, every.offset, [[0, KH], [1, Q * B]])
                sp.dma_start(hot_ids_in[n % 2], every).then_inc(hot_ids_arrived[n % 2], 16)

            sp.dma_start(ids[:], ids_t).then_inc(ids_in, 16)
            hot(0)
            sp.dma_start(row_of[:], hot_rows).then_inc(row_of_in, 16)
            hot(1)
            sp.dma_start(pick_in[:], pick_c).then_inc(consts_in, 16)
            raw(0)
            sp.dma_start(ident[:], ident_c).then_inc(consts_in, 16)
            sp.dma_start(select[:], select_c).then_inc(consts_in, 16)
            raw(1)
            loaded = 0
            for step in STEPS:
                if step[0] == "weights":
                    i = step[1]
                    sp.wait_ge(w_high, i + 1)
                    sp.wait_ge(w_low, i + 1)
                    sp.dma_start(w_split[i].rearrange("s p x -> p s x"),
                                 w_parts[:, i % WBUF].bitcast(fp32)).then_inc(w_saved[i % WBUF], 16)
                    if i + WBUF < NPIECE:
                        raw(i + WBUF)
                    if loaded < min(i, WRING):
                        load(loaded)
                        loaded += 1
                elif step[0] == "chunk":
                    if WRING <= loaded < NPIECE and FIRST_PART[step[1]] >= PIECE * (loaded - WRING + 1):
                        load(loaded)
                        loaded += 1
                    if step[1] == TOP_AT:
                        sp.wait_ge(hot_ids_ready, NHOT)
                        for tile, source in ((w1, w1_z), (w1d, w1_dense), (dense, dense_t), (w2, w2_t), (w3, w3_t),
                                             (b1, b1_t), (b2, b2_t)):
                            sp.dma_start(tile[:], source).then_inc(top_in, 16)
            sp.wait_ge(y_ready, 1)
            sp.dma_start(out.rearrange("b o -> o b"), y).then_inc(y_stored, 16)
            sp.wait_ge(y_stored, 16)

        @block.scalar
        def _(act):
            z_taken = 0
            top_waited = False

            def take_z():
                nonlocal z_taken
                last = min(ROWS_T // Q * (z_taken + 1), NBATCH)
                act.wait_ge(summed, last)
                nc.scalar.copy(z[:, z_taken, :], z_ps[:]).then_inc(z_out, 1)
                z_taken += 1

            for step in STEPS:
                if step[0] == "weights":
                    i = step[1]
                    act.wait_ge(w_raw_in[i % WBUF], 16 * (i // WBUF + 1))
                    if i >= WBUF:
                        act.wait_ge(w_saved[i % WBUF], 16 * (i // WBUF))
                    nc.scalar.copy(w_parts[:, i % WBUF, 0, :], w_raw[:, i % WBUF, :]).then_inc(w_high, 1)
                elif step[0] == "split":
                    f = step[1]
                    act.wait_ge(gathered[f], 16 * BT)
                    if f >= Q * NHOT + EHL:
                        act.wait_ge(spare_filled, USE["feature", f - EHL] + 1)
                    nc.scalar.copy(e_parts[:, f % EHL, :, :, 0, :], rows_twice(f)).then_inc(e_high, 1)
                elif step[0] == "feature":
                    f = step[1]
                    act.wait_ge(spare_filled, USE[step] + 1)
                    nc.scalar.copy(e_stack(f), spare[:]).then_inc(spare_out, 1)
                elif step[0] == "table":
                    n = step[1]
                    act.wait_ge(table_in[n], 16 * Q)
                    if n >= 2:
                        act.wait_ge(onehot_used, sum(J[:n - 1]))
                    part = [table_parts[:, n % 2, i, :, 0:J[n], :] for i in range(3)]
                    nc.scalar.copy(part[0], table[:, n, :, 0:J[n], :]).then_inc(table_high, 1)
                    act.wait_ge(table_rest, n + 1)
                    nc.scalar.copy(part[1], table[:, n, :, 0:J[n], :]).then_inc(table_mid, 1)
                elif step[0] == "picked":
                    n = step[1]
                    act.wait_ge(onehot_used, sum(J[:n + 1]))
                    nc.scalar.copy(e_blk[:, n, :], z_ps[:]).then_inc(picked_out, 1)
                    act.wait_ge(picked_out, n + 1)
                    if n:
                        act.wait_ge(spare_filled, USE["feature", Q * n - 1] + 1)
                    nc.scalar.copy(e_high_t[:], e_blk[:, n, :]).then_inc(hot_high, 1)
                elif step[0] == "block":
                    n = step[1]
                    rows = min(F - Q * n, Q) * D
                    act.wait_ge(spare_filled, USE[step] + 1)
                    nc.scalar.copy(e_blk[0:rows, n, :], spare[0:rows, :]).then_inc(spare_out, 1)
                elif step[0] == "layer1" and step[1] == 0:
                    m = step[2]
                    if not top_waited:
                        act.wait_ge(top_in, 16 * 7)
                        top_waited = True
                    act.wait_ge(spare_filled, USE[step] + 1)
                    nc.scalar.activation(h1[:, m, :], spare[:], ACT.Identity, bias=b1[:, m:m + 1]).then_inc(spare_out, 1)
                elif step[0] == "chunk":
                    if z_taken < KT - 1 and step[1] >= last_chunk_of(ROWS_T // Q * (z_taken + 1) - 1) + 3:
                        take_z()
            while z_taken < KT:
                take_z()
            for m in range(H1 // P):
                act.wait_ge(h1_added, m + 1)
                nc.scalar.activation(h1[:, m, :], h1[:, m, :], ACT.Relu).then_inc(h1_ready, 1)
            for m in range(H2 // P):
                act.wait_ge(h2_sum, m + 1)
                nc.scalar.activation(h2[:, m, :], h2_ps[m], ACT.Relu, bias=b2[:, m:m + 1]).then_inc(h2_ready, 1)
            act.wait_ge(y_sum, 1)
            nc.scalar.copy(y, y_ps).then_inc(y_ready, 1)

        @block.vector
        def _(dve):
            dve.wait_ge(pad_zeroed, 1)
            for step in STEPS:
                if step[0] == "table":
                    n = step[1]
                    dve.wait_ge(hot_ids_arrived[n % 2], 16 * (n // 2 + 1))
                    nc.vector.tensor_copy(hot_ids_16[:, n % 2, :], hot_ids_in[n % 2]).then_inc(hot_ids_ready, 1)
                    part = [table_parts[:, n % 2, i, :, 0:J[n], :] for i in range(3)]
                    rest = table[:, n, :, 0:J[n], :]
                    dve.wait_ge(table_high, n + 1)
                    nc.vector.tensor_tensor(rest, rest, part[0], ALU.subtract).then_inc(table_rest, 1)
                    dve.wait_ge(table_mid, n + 1)
                    nc.vector.tensor_tensor(part[2], rest, part[1], ALU.subtract).then_inc(table_low, 1)
                elif step[0] == "slice":
                    n, j = step[1:]
                    if (n, j) == (0, 0):
                        dve.wait_ge(row_of_in, 16)
                    dve.wait_ge(hot_ids_ready, n + 1)
                    at = sum(J[:n]) + j
                    if at >= KT // 2:
                        dve.wait_ge(onehot_used, at - KT // 2 + 1)
                    nc.vector.tensor_scalar(onehot[:, at % (KT // 2), :], hot_ids_16[:, n % 2, :],
                                            row_of[:, n * JMAX + j:n * JMAX + j + 1], None,
                                            ALU.is_equal).then_inc(onehot_ready, 1)
                elif step[0] == "picked":
                    n = step[1]
                    if n == 0:
                        dve.wait_ge(consts_in, 16 * 3)
                        nc.vector.tensor_copy(ident_r[:], ident[:])
                        nc.vector.tensor_copy(pick[:], pick_in[:]).then_inc(pick_ready, 1)
                    dve.wait_ge(hot_high, n + 1)
                    nc.vector.tensor_tensor(e_low_t[:], e_blk[:, n, :], e_high_t[:].bitcast(fp32),
                                            ALU.subtract).then_inc(hot_low, 1)
                elif step[0] == "weights":
                    i = step[1]
                    dve.wait_ge(w_high, i + 1)
                    nc.vector.tensor_tensor(w_parts[:, i % WBUF, 1, :], w_raw[:, i % WBUF, :],
                                            w_parts[:, i % WBUF, 0, :].bitcast(fp32), ALU.subtract).then_inc(w_low, 1)
                elif step[0] == "split":
                    f = step[1]
                    dve.wait_ge(e_high, f - Q * NHOT + 1)
                    nc.vector.tensor_tensor(e_parts[:, f % EHL, :, :, 1, :], rows_twice(f),
                                            e_parts[:, f % EHL, :, :, 0, :].bitcast(fp32), ALU.subtract).then_inc(e_low, 1)
                elif step[0] == "chunk":
                    k = step[1]
                    tiles = CHUNKS[k][1]
                    first, n = tiles[0][0], len(tiles)
                    by = e_blk[:, first:first + 2, :]
                    if tiles[-1][0] == first:
                        by = e_blk[:, first:first + 1, :].to_broadcast([P, n, B])
                    dve.wait_ge(t_ready, k + 1)
                    if tiles[-1][0] < NHOT:
                        dve.wait_ge(picked_out, tiles[-1][0] + 1)
                    else:
                        dve.wait_ge(spare_out, USE["block", tiles[-1][0]] + 1)
                    if k >= PRODS:
                        dve.wait_ge(summed, batch_of(FIRST_TILE[k - PRODS + 1] - 1) + 1)
                    nc.vector.tensor_tensor(prod[:, k % PRODS, 0:n, :], t_ps[k % TBUF][:, 0:n, :], by,
                                            ALU.mult).then_inc(prod_ready, 1)
                elif step[0] == "layer1" and step[1] > 0:
                    m = step[2]
                    dve.wait_ge(spare_filled, USE[step] + 1)
                    nc.vector.tensor_tensor(h1[:, m, :], spare[:], h1[:, m, :], ALU.add).then_inc(spare_out, 1)
            for m in range(H1 // P):
                dve.wait_ge(h1_sum, m + 1)
                nc.vector.tensor_tensor(h1[:, m, :], h1_ps[m], h1[:, m, :], ALU.add).then_inc(h1_added, 1)

        @block.tensor
        def _(pe):
            batches = 0

            def sums(upto):
                nonlocal batches
                while batches < NBATCH and last_chunk_of(batches) < upto:
                    b = batches
                    pe.wait_ge(prod_ready, last_chunk_of(b) + 1)
                    per = ROWS_T // Q
                    if b == 0:
                        pe.wait_ge(picked_out, NHOT)
                    elif b % per == 0:
                        pe.wait_ge(z_out, b // per)
                    for t in range(Q * b, min(Q * b + Q, NT)):
                        k = next(k for k in range(len(CHUNKS)) if FIRST_TILE[k + 1] > t)
                        g, at = t % Q, Q * (b % per)
                        last = nc.tensor.matmul(z_ps[D * g:D * (g + 1), :], select[:, D - Q - at:2 * D - Q - at],
                                                prod[:, k % PRODS, t - FIRST_TILE[k], :],
                                                start=(b % per == 0), stop=(b % per == per - 1 or t + Q >= NT))
                    last.then_inc(summed, 1)
                    batches += 1

            def spare_free(step):
                if USE[step]:
                    pe.wait_ge(spare_out, USE[step])

            stacks = 0
            top_waited = False
            for step in STEPS:
                if step[0] == "slice":
                    n, j = step[1:]
                    pe.wait_ge(table_low, n + 1)
                    if n and j == 0:
                        pe.wait_ge(picked_out, n)
                    at = sum(J[:n]) + j
                    pe.wait_ge(onehot_ready, at + 1)
                    for i in range(3):
                        for q in range(Q):
                            last = nc.tensor.matmul(z_ps[D * q:D * (q + 1), :], table_parts[:, n % 2, i, q, j, :],
                                                    onehot[:, at % (KT // 2), q * B:(q + 1) * B],
                                                    start=(j == 0 and i == 0), stop=(j == J[n] - 1 and i == 2))
                    last.then_inc(onehot_used, 1)
                elif step[0] == "feature" and step[1] < Q * NHOT:
                    f = step[1]
                    if f == 0:
                        pe.wait_ge(pick_ready, 1)
                    pe.wait_ge(hot_low, f // Q + 1)
                    spare_free(step)
                    rows = slice(D * (f % Q), D * (f % Q + 1))
                    nc.tensor.matmul(spare[:], pick[rows, 0, :], e_high_t[rows, :], start=True, stop=False)
                    nc.tensor.matmul(spare[:], pick[rows, 1, :], e_low_t[rows, :], start=False,
                                     stop=True).then_inc(spare_filled, 1)
                elif step[0] == "feature":
                    f = step[1]
                    pe.wait_ge(e_low, f - Q * NHOT + 1)
                    spare_free(step)
                    for bt in range(BT):
                        parts = e_parts[:, f % EHL, bt].rearrange("p r s x -> p (r s x)")
                        last = nc.tensor.matmul(spare[:, bt * P:(bt + 1) * P], parts, ident_r[:], start=True, stop=True)
                    last.then_inc(spare_filled, 1)
                elif step[0] == "block":
                    n = step[1]
                    fs = min(F - Q * n, Q)
                    spare_free(step)
                    for bt in range(BT):
                        last = nc.tensor.transpose(spare[0:fs * D, bt * P:(bt + 1) * P],
                                                   e_nat[:, n % NAT, bt, 0:fs, :].rearrange("p f x -> p (f x)"), ident[:])
                    last.then_inc(spare_filled, 1)
                elif step[0] == "layer1":
                    use, m = step[1:]
                    cols = slice(m * P, (m + 1) * P)
                    if not top_waited:
                        pe.wait_ge(top_in, 16 * 7)
                        top_waited = True
                    spare_free(step)
                    pe.wait_ge(z_out, FLUSH[use])
                    kts = range(FLUSH[use - 1] if use else 0, FLUSH[use])
                    if use == 0:
                        nc.tensor.matmul(spare[:], w1d[:, cols], dense[:], start=True, stop=False)
                    for kt in kts:
                        last = nc.tensor.matmul(spare[:], w1[:, kt, cols], z[:, kt, :],
                                                start=(use > 0 and kt == kts[0]), stop=(kt == kts[-1]))
                    last.then_inc(spare_filled, 1)
                elif step[0] == "chunk":
                    k = step[1]
                    sums(k - TBUF + 1)
                    if k >= TBUF:
                        pe.wait_ge(prod_ready, k - TBUF + 1)
                    part = FIRST_PART[k]
                    for n, (m, parts) in enumerate(CHUNKS[k][1]):
                        for at, (f, qs) in enumerate(parts):
                            i = part // PIECE
                            if part % PIECE == 0:
                                pe.wait_ge(w_loaded[i % WRING], 32 * (i // WRING + 1))
                            if USE["feature", f] + 1 > stacks:
                                stacks = USE["feature", f] + 1
                                pe.wait_ge(spare_out, stacks)
                            last = nc.tensor.matmul(t_ps[k % TBUF][:, n, :], w_ring[:, i % WRING, part % PIECE, :],
                                                    e_stack(f), start=(at == 0), stop=(at == len(parts) - 1))
                            part += 1
                    last.then_inc(t_ready, 1)
            sums(len(CHUNKS))

            pe.wait_ge(z_out, KT)
            for m in range(H1 // P):
                for kt in range(FLUSH[-1], KT):
                    last = nc.tensor.matmul(h1_ps[m], w1[:, kt, m * P:(m + 1) * P], z[:, kt, :],
                                            start=(kt == FLUSH[-1]), stop=(kt == KT - 1))
                last.then_inc(h1_sum, 1)
            for kt in range(H1 // P):
                pe.wait_ge(h1_ready, kt + 1)
                for m in range(H2 // P):
                    last = nc.tensor.matmul(h2_ps[m], w2[:, kt, m * P:(m + 1) * P], h1[:, kt, :],
                                            start=(kt == 0), stop=(kt == H1 // P - 1))
                    if kt == H1 // P - 1:
                        last.then_inc(h2_sum, 1)
            for m in range(H2 // P):
                pe.wait_ge(h2_ready, m + 1)
                last = nc.tensor.matmul(y_ps, w3[:, m:m + 1], h2[:, m, :], start=(m == 0), stop=(m == H2 // P - 1))
            last.then_inc(y_sum, 1)


def lay_out(inputs):
    import numpy as np

    def array(name):
        return np.ascontiguousarray(inputs[name])

    arrays = {f"tbl_{f}": array(f"tbl_{f}") for f in range(F)}
    ids = array("ids")[:, ORDER]
    arrays["hot_ids"] = np.ascontiguousarray(ids.T[:Q * NHOT].reshape(NHOT, Q * B))
    arrays["ids"] = np.ascontiguousarray(ids.reshape(BT, P, F).transpose(1, 2, 0)[:, Q * NHOT:].reshape(P, -1))
    arrays["dense"] = np.ascontiguousarray(array("dense_ctx").T)
    w = array("L0_rec_w")
    parts = np.zeros((D, NPIECE * PIECE, Q, D), w.dtype)
    for n, (m, f, qs) in enumerate(PARTS):
        for q in qs:
            a, b = ORDER[f], ORDER[Q * m + q]
            parts[:, n, q, :] = w[:, pair_index(b, a), :] if b < a else w[:, pair_index(a, b), :].T
    arrays["w"] = np.ascontiguousarray(parts.reshape(D, NPIECE, Q * WC).transpose(1, 0, 2).reshape(NPIECE, P, WC))
    w1 = array("W_top1")
    w1_z = np.zeros((P, KT, H1), w1.dtype)
    for t, (m, parts_) in enumerate(TILES):
        kt = z_row(t, 0)[0]
        for f, qs in parts_:
            for q in qs:
                a, b = ORDER[f], ORDER[Q * m + q]
                w1_z[z_row(t, q)[1], kt] = w1[pair_index(min(a, b), max(a, b))]
    arrays["w1_z"] = w1_z
    arrays["w1_dense"] = np.ascontiguousarray(w1[NPAIR:])
    arrays["b1"] = np.ascontiguousarray(array("b_top1").reshape(H1 // P, P).T)
    arrays["w2"] = np.ascontiguousarray(array("W_top2").reshape(H1 // P, P, H2).transpose(1, 0, 2))
    arrays["b2"] = np.ascontiguousarray(array("b_top2").reshape(H2 // P, P).T)
    arrays["w3"] = np.ascontiguousarray(array("W_top3").reshape(H2 // P, P).T)
    arrays["ident"] = np.eye(P, dtype=np.float32)
    select = np.zeros((P, 2 * D - Q), np.float32)
    for q in range(Q):
        select[D * q:D * (q + 1), D - Q + q] = 1.0
    arrays["select"] = select
    row_of = np.zeros((KH, NHOT, JMAX), np.float32)
    for n in range(NHOT):
        row_of[:, n, :J[n]] = np.arange(KH * J[n]).reshape(KH, J[n])
    arrays["hot_rows"] = row_of.reshape(KH, NHOT * JMAX)
    pick = np.zeros((Q, D, 2, 2, 2, D), np.float32)
    for s in range(2):
        for x in range(D):
            pick[:, x, s, :, s, x] = 1.0
    arrays["pick"] = pick.reshape(P, 2, P)
    return arrays


def kernel(**inputs):
    import concourse.bacc as _bacc
    from concourse import mybir as _mybir
    from concourse.bass_utils import run_bass_kernel_spmd as _run

    nc = _bacc.Bacc("TRN2", target_bir_lowering=False, num_devices=1)
    arrays = {f"in_{name}": a for name, a in lay_out(inputs).items()}
    aps = {name: nc.dram_tensor(name, a.shape, _mybir.dt.from_np(a.dtype), kind="ExternalInput").ap()
           for name, a in arrays.items()}
    out = nc.dram_tensor("out_y", (B, 1), _mybir.dt.float32, kind="ExternalOutput").ap()
    tower(nc, aps["in_dense"], aps["in_ids"], [aps[f"in_tbl_{f}"] for f in range(F)],
          aps["in_hot_ids"], aps["in_hot_rows"], aps["in_pick"], aps["in_w"], aps["in_w1_z"],
          aps["in_w1_dense"], aps["in_b1"], aps["in_w2"], aps["in_b2"], aps["in_w3"], aps["in_ident"],
          aps["in_select"], out)
    r = _run(nc, [arrays], core_ids=[0])
    return r.results[0]["out_y"]
```

```python
import concourse.bass as bass
from concourse import mybir
from contextlib import ExitStack

F = 39
D = 32
B = 512
P = 128
BT = B // P
Q = P // D
NBLK = (F + Q - 1) // Q
ROWS = [125000, 1000, 1250, 1000, 1250, 1250, 12500, 1250, 1250, 125000, 1250, 12500, 1250, 12500, 12500, 125000, 1250,
        1000, 125000, 125000, 1250, 1250, 12500, 1250, 1000, 12500, 1000, 12500, 1000, 125000, 1000, 12500, 1250, 1250,
        1000, 1250, 12500, 12500, 1000]
KH = 125
ORDER = sorted(range(F), key=lambda f: ROWS[f])[:Q]
ORDER += [f for f in range(F) if f not in ORDER]
J = max(ROWS[f] for f in ORDER[:Q]) // KH
NPAIR = F * (F - 1) // 2
DENSE = 16
H1, H2 = 512, 256


def pair_index(i, j):
    return i * F - i * (i + 1) // 2 + (j - i - 1)


def plan():
    chunks = []
    for f in range(F):
        n = f // Q
        cross = [(m, [(f, tuple(range(Q)))]) for m in range(n)]
        for m in range(0, n - 1, 2):
            chunks.append((f, cross[m:m + 2]))
        if n % 2:
            if f % 2:
                chunks.append((f, [(n - 1, [(f - 1, tuple(range(Q)))]), cross[n - 1]]))
            elif f == F - 1:
                chunks.append((f, [cross[n - 1], (n, [(Q * n + 1, (0,)), (Q * n + 2, (1,)), (Q * n, (2,))])]))
        if f % Q == Q - 1:
            a = Q * n
            chunks.append((f, [(n, [(a + 1, (0, 2, 3))]), (n, [(a + 2, (0,)), (a, (3,)), (a + 3, (2,))])]))
    return chunks


CHUNKS = plan()
TILES = [t for _, tiles in CHUNKS for t in tiles]
PARTS = [(m, f, qs) for m, parts in TILES for f, qs in parts]
NT, NW = len(TILES), len(PARTS)
FIRST_TILE = [sum(len(t) for _, t in CHUNKS[:k]) for k in range(len(CHUNKS) + 1)]
FIRST_PART = [sum(len(p) for _, t in CHUNKS[:k] for _, p in t) for k in range(len(CHUNKS) + 1)]
PIECE = 15
NPIECE = (NW + PIECE - 1) // PIECE
WC = PIECE * P // Q
ROWS_T = P // Q
KT = (NT + ROWS_T - 1) // ROWS_T
NBATCH = (NT + Q - 1) // Q
TBUF, WRING, EHL, NAT = 3, 3, 3, 3
PRODS = 5
NFIRST = 21
FLUSH = (1, 3, 5)


def z_row(t, q):
    return t // ROWS_T, D * (t % Q) + Q * ((t % ROWS_T) // Q) + q


def batch_of(t):
    return t // Q


def last_chunk_of(batch):
    last = min(Q * batch + Q, NT) - 1
    return next(k for k in range(len(CHUNKS)) if FIRST_TILE[k + 1] > last)


def layer1_operands(use):
    return [-1, *range(FLUSH[0])] if use == 0 else [*range(FLUSH[use - 1], FLUSH[use])]


def steps():
    out = [("table",), ("onehot", 0), ("table low",), ("onehot", 1)]
    for j in range(J):
        if j + 2 < J:
            out.append(("onehot", j + 2))
        out.append(("slice", j))
        if j == 0:
            out.append(("consts",))
    out += [("weights", 0), ("picked",), ("weights", 1), ("hot low",)]
    piece = 2
    layer1 = [(use, m) for use in range(len(FLUSH)) for m in range(H1 // P)]

    def layer1_from(unit):
        use, m = unit
        start, end = (last_chunk_of(z * ROWS_T // Q - 1) + 5 for z in (*FLUSH, KT)[use:use + 2])
        return start + (end - start) * m // (H1 // P)

    first_use = [next((k for k, c in enumerate(CHUNKS) if any(g == f for _, p in c[1] for g, _ in p)), len(CHUNKS))
                 for f in range(F)]
    need = [min(first_use[f:]) for f in range(F)]
    blocks = []
    products = 0
    split, stack = Q, 0

    def layer1_step():
        nonlocal products
        unit = layer1[0]
        if products + 1 < len(layer1_operands(unit[0])):
            out.append(("product", *unit, products))
            products += 1
        else:
            out.append(("layer1", *layer1.pop(0)))
            products = 0

    def stacked():
        nonlocal stack
        while products:
            layer1_step()
        while blocks:
            out.append(blocks.pop())
        out.append(("feature", stack))
        stack += 1
        if stack > Q and (stack % Q == 0 or stack == F):
            blocks.append(("block", (stack - 1) // Q))

    for k in range(len(CHUNKS)):
        while split < F and need[split] <= k + AHEAD_SPLIT:
            if split - stack >= EHL - 1:
                stacked()
            else:
                out.append(("split", split))
                split += 1
        while stack < F and need[stack] <= k + AHEAD_STACK:
            stacked()
        if piece < NPIECE and k % W_CHUNKS == 0:
            out.append(("weights", piece))
            piece += 1
        out.append(("chunk", k))
        if blocks:
            out.append(blocks.pop())
        elif products:
            layer1_step()
        elif layer1 and k >= layer1_from(layer1[0]):
            rest = len(layer1_operands(layer1[0][0])) - 1
            if stack == F or need[stack] > k + AHEAD_STACK + rest + 1 or k >= layer1_from(layer1[0]) + PATIENCE:
                layer1_step()
    while layer1:
        layer1_step()
    return out


TOP_AT = 5
W_CHUNKS = 3
WBUF = 2
AHEAD_SPLIT = 5
AHEAD_STACK = 3
PATIENCE = 5
STEPS = steps()
SPARE = [s for s in STEPS if s[0] in ("feature", "block", "layer1")]
USE = {s: n for n, s in enumerate(SPARE)}
EARLY = sum(s in USE for s in STEPS[:STEPS.index(("chunk", 0))])


def bank_of(n):
    return 0 if n >= EARLY else n % (1 + 2 * TBUF)


def use_before(n):
    return max((m for m in range(n) if bank_of(m) == bank_of(n)), default=None)


def tower(nc, dense_t, ids_t, tables, hot_ids, hot_rows, pick_c, w_dense, w1_z, w1_dense, b1_t, w2_t, b2_t, w3_t,
          ident_c, select_c, out):
    fp32 = mybir.dt.float32
    fp32r = mybir.dt.float32r
    bf16 = mybir.dt.bfloat16
    fp16 = mybir.dt.float16
    int32 = mybir.dt.int32
    ALU = mybir.AluOpType
    ACT = mybir.ActivationFunctionType
    w_split = nc.dram_tensor("w_split", (NPIECE, 2, P, WC), fp32, kind="Internal").ap()

    ctx = ExitStack()
    with ctx:
        def sb(name, shape, dt=fp32):
            return ctx.enter_context(nc.sbuf_tensor(name, shape, dt))

        def sem(name):
            return ctx.enter_context(nc.semaphore(name))

        ids = sb("ids_sb", [P, (F - Q) * BT], int32)
        e_nat = sb("e_nat", [P, NAT, BT, Q, D])
        e_parts = sb("e_parts", [P, EHL, BT, 2, 2, D], fp32r)
        e_stack_first = sb("e_stack_first", [P, NFIRST, B], fp32r)
        e_blk = sb("e_blk", [P, NBLK, B])
        w_raw = sb("w_raw", [P, WBUF, WC])
        w_parts = sb("w_parts", [P, WBUF, 2, WC], fp32r)
        w_ring = sb("w_ring", [P, WRING, PIECE, P], fp32r)
        prod = sb("prod", [P, PRODS, 2, B])
        z = sb("z", [P, KT, B])
        w1 = sb("w1", [P, KT, H1])
        w1d = sb("w1d", [DENSE, H1])
        dense = sb("dense", [DENSE, B])
        w2 = sb("w2", [P, H1 // P, H2])
        w3 = sb("w3", [P, H2 // P])
        b1 = sb("b1", [P, H1 // P])
        b2 = sb("b2", [P, H2 // P])
        h1 = sb("h1", [P, H1 // P, B])
        h2 = prod[:, 0]
        y = prod[0:1, 1, 0, :]
        ident = sb("ident", [P, P])
        select = sb("select", [P, 2 * D - Q])
        ident_r = sb("ident_r", [P, P], fp32r)
        with ExitStack() as early:
            def early_sb(name, shape, dt):
                return early.enter_context(nc.sbuf_tensor(name, shape, dt))

            table = early_sb("table", [KH, Q, J, D], fp32)
            table_parts = early_sb("table_parts", [KH, 3, Q, J, D], bf16)
            hot_ids_16 = early_sb("hot_ids_16", [KH, Q * B], fp16)
            row_of = early_sb("row_of", [KH, J], fp32)
            pick_in = early_sb("pick_in", [P, 2, P], fp32)
            pick = early_sb("pick", [P, 2, P], fp32r)
            e_high_t = early_sb("e_high_t", [P, B], fp32r)
            e_low_t = early_sb("e_low_t", [P, B], fp32r)
        e_stack_late = sb("e_stack_late", [P, F - NFIRST, B], fp32r)
        hot_ids_in = h1[0:KH].rearrange("p a b -> p (a b)").bitcast(int32)
        onehot = z[0:KH].rearrange("p a b -> p (a b)").bitcast(bf16).rearrange("p (a b) -> p a b", a=KT // 2)

        def e_stack(f):
            return e_stack_first[:, f, :] if f < NFIRST else e_stack_late[:, f - NFIRST, :]

        t_ps = [ctx.enter_context(nc.psum_tensor(f"t_ps{i}", [P, 2, B], fp32)) for i in range(TBUF)]
        z_ps = ctx.enter_context(nc.psum_tensor("z_ps", [P, B], fp32))
        spare = ctx.enter_context(nc.psum_tensor("spare", [P, B], fp32))
        h1_ps = [t_ps[m // 2][:, m % 2, :] for m in range(H1 // P)]
        h2_ps = [t_ps[2][:, m, :] for m in range(H2 // P)]
        y_ps = z_ps[0:1, :]

        ids_in = sem("ids_in")
        row_of_in = sem("row_of_in")
        consts_in = sem("consts_in")
        top_in = sem("top_in")
        table_in = sem("table_in")
        hot_ids_arrived = sem("hot_ids_arrived")
        pick_ready = sem("pick_ready")
        table_high = sem("table_high")
        table_rest = sem("table_rest")
        table_mid = sem("table_mid")
        table_low = sem("table_low")
        hot_ids_ready = sem("hot_ids_ready")
        onehot_ready = sem("onehot_ready")
        onehot_used = sem("onehot_used")
        picked_out = sem("picked_out")
        hot_high = sem("hot_high")
        hot_low = sem("hot_low")
        gathered = [sem(f"gathered{f}") for f in range(F)]
        pad_zeroed = sem("pad_zeroed")
        e_high = sem("e_high")
        e_low = sem("e_low")
        spare_filled = sem("spare_filled")
        spare_out = sem("spare_out")
        w_raw_in = [sem(f"w_raw_in{i}") for i in range(WBUF)]
        w_high = sem("w_high")
        w_low = sem("w_low")
        w_saved = [sem(f"w_saved{i}") for i in range(WBUF)]
        w_loaded = [sem(f"w_loaded{i}") for i in range(WRING)]
        t_ready = sem("t_ready")
        prod_ready = sem("prod_ready")
        summed = sem("summed")
        z_out = sem("z_out")
        h1_sum = sem("h1_sum")
        h1_added = sem("h1_added")
        h1_ready = sem("h1_ready")
        h2_sum = sem("h2_sum")
        h2_ready = sem("h2_ready")
        y_sum = sem("y_sum")
        y_ready = sem("y_ready")
        y_stored = sem("y_stored")

        def bank(step):
            at = bank_of(USE[step]) - 1
            return spare[:] if at < 0 else t_ps[at // 2][:, at % 2, :]

        def rows_twice(f):
            rows = e_nat[:, f // Q % NAT, :, f % Q, :]
            return bass.AP(rows.tensor, rows.offset, [rows.ap[0], rows.ap[1], [0, 2], rows.ap[2]])

        block = ctx.enter_context(nc.Block())

        @block.gpsimd
        def _(pool):
            nc.gpsimd.memset(e_blk[P - D:P, NBLK - 1, :], 0.0).then_inc(pad_zeroed, 1)
            pool.wait_ge(ids_in, 16)

            def gather(f):
                if f % Q == 0 and f // Q > NAT:
                    pool.wait_ge(spare_filled, USE["block", f // Q - NAT] + 1)
                for bt in range(BT):
                    at = (f - Q) * BT + bt
                    pool.indirect_dma_start(
                        out=e_nat[:, f // Q % NAT, bt, f % Q, :], out_offset=None, in_=tables[ORDER[f]],
                        in_offset=bass.IndirectOffsetOnAxis(ap=ids[:, at:at + 1], axis=0),
                    ).then_inc(gathered[f], 16)

            for f in range(Q, F):
                gather(f)

        @block.sync
        def _(sp):
            def raw(i):
                sp.dma_start(w_raw[:, i % WBUF, :], w_dense[i]).then_inc(w_raw_in[i % WBUF], 16)

            def load(i):
                sp.wait_ge(w_saved[i % WBUF], 16 * (i // WBUF + 1))
                if i >= WRING:
                    last = PIECE * (i - WRING + 1)
                    sp.wait_ge(t_ready, next(k for k in range(len(CHUNKS)) if FIRST_PART[k + 1] >= last) + 1)
                for s in range(2):
                    piece = w_split[i, s]
                    twice = bass.AP(piece.tensor, piece.offset, [[0, 2], [Q * WC, D], [1, Q * WC]])
                    sp.dma_start(w_ring[2 * D * s:2 * D * (s + 1), i % WRING].bitcast(fp32).rearrange("p a b -> p (a b)"),
                                 twice).then_inc(w_loaded[i % WRING], 16)

            sp.dma_start(ids[:], ids_t).then_inc(ids_in, 16)
            for q in range(Q):
                sp.dma_start(table[:, q], tables[ORDER[q]].rearrange("(p j) x -> p j x", p=KH)).then_inc(table_in, 16)
            every = bass.AP(hot_ids.tensor, hot_ids.offset, [[0, KH], [1, Q * B]])
            sp.dma_start(hot_ids_in, every).then_inc(hot_ids_arrived, 16)
            sp.dma_start(row_of[:], hot_rows).then_inc(row_of_in, 16)
            sp.dma_start(pick_in[:], pick_c).then_inc(consts_in, 16)
            sp.dma_start(ident[:], ident_c).then_inc(consts_in, 16)
            sp.dma_start(select[:], select_c).then_inc(consts_in, 16)
            raw(0)
            raw(1)
            loaded = 0
            for step in STEPS:
                if step[0] == "weights":
                    i = step[1]
                    sp.wait_ge(w_high, i + 1)
                    sp.wait_ge(w_low, i + 1)
                    sp.dma_start(w_split[i].rearrange("s p x -> p s x"),
                                 w_parts[:, i % WBUF].bitcast(fp32)).then_inc(w_saved[i % WBUF], 16)
                    if i + WBUF < NPIECE:
                        raw(i + WBUF)
                    if loaded < min(i, WRING):
                        load(loaded)
                        loaded += 1
                elif step[0] == "chunk":
                    if WRING <= loaded < NPIECE and FIRST_PART[step[1]] >= PIECE * (loaded - WRING + 1):
                        load(loaded)
                        loaded += 1
                    if step[1] == TOP_AT:
                        for tile, source in ((w1, w1_z), (w1d, w1_dense), (dense, dense_t), (w2, w2_t), (w3, w3_t),
                                             (b1, b1_t), (b2, b2_t)):
                            sp.dma_start(tile[:], source).then_inc(top_in, 16)
            sp.wait_ge(y_ready, 1)
            sp.dma_start(out.rearrange("b o -> o b"), y).then_inc(y_stored, 16)
            sp.wait_ge(y_stored, 16)

        @block.scalar
        def _(act):
            z_taken = 0
            top_waited = False

            def take_z():
                nonlocal z_taken
                last = min(ROWS_T // Q * (z_taken + 1), NBATCH)
                act.wait_ge(summed, last)
                nc.scalar.copy(z[:, z_taken, :], z_ps[:]).then_inc(z_out, 1)
                z_taken += 1

            for step in STEPS:
                if step[0] == "weights":
                    i = step[1]
                    act.wait_ge(w_raw_in[i % WBUF], 16 * (i // WBUF + 1))
                    if i >= WBUF:
                        act.wait_ge(w_saved[i % WBUF], 16 * (i // WBUF))
                    nc.scalar.copy(w_parts[:, i % WBUF, 0, :], w_raw[:, i % WBUF, :]).then_inc(w_high, 1)
                elif step[0] == "split":
                    f = step[1]
                    act.wait_ge(gathered[f], 16 * BT)
                    if f - Q >= EHL:
                        act.wait_ge(spare_filled, USE["feature", f - EHL] + 1)
                    nc.scalar.copy(e_parts[:, f % EHL, :, :, 0, :], rows_twice(f)).then_inc(e_high, 1)
                elif step[0] == "feature":
                    f = step[1]
                    act.wait_ge(spare_filled, USE[step] + 1)
                    nc.scalar.copy(e_stack(f), bank(step)).then_inc(spare_out, 1)
                elif step[0] == "table":
                    act.wait_ge(table_in, 16 * Q)
                    nc.scalar.copy(table_parts[:, 0], table[:]).then_inc(table_high, 1)
                    act.wait_ge(table_rest, 1)
                    nc.scalar.copy(table_parts[:, 1], table[:]).then_inc(table_mid, 1)
                elif step[0] == "picked":
                    act.wait_ge(onehot_used, J)
                    nc.scalar.copy(e_blk[:, 0, :], z_ps[:]).then_inc(picked_out, 1)
                    nc.scalar.copy(e_high_t[:], z_ps[:]).then_inc(hot_high, 1)
                elif step[0] == "block":
                    n = step[1]
                    rows = min(F - Q * n, Q) * D
                    act.wait_ge(spare_filled, USE[step] + 1)
                    nc.scalar.copy(e_blk[0:rows, n, :], bank(step)[0:rows, :]).then_inc(spare_out, 1)
                elif step[0] == "layer1" and step[1] == 0:
                    m = step[2]
                    if not top_waited:
                        act.wait_ge(top_in, 16 * 7)
                        top_waited = True
                    act.wait_ge(spare_filled, USE[step] + 1)
                    nc.scalar.activation(h1[:, m, :], spare[:], ACT.Identity, bias=b1[:, m:m + 1]).then_inc(spare_out, 1)
                elif step[0] == "chunk":
                    if z_taken < KT - 1 and step[1] >= last_chunk_of(ROWS_T // Q * (z_taken + 1) - 1) + 3:
                        take_z()
            while z_taken < KT:
                take_z()
            for m in range(H1 // P):
                act.wait_ge(h1_added, m + 1)
                nc.scalar.activation(h1[:, m, :], h1[:, m, :], ACT.Relu).then_inc(h1_ready, 1)
            for m in range(H2 // P):
                act.wait_ge(h2_sum, m + 1)
                nc.scalar.activation(h2[:, m, :], h2_ps[m], ACT.Relu, bias=b2[:, m:m + 1]).then_inc(h2_ready, 1)
            act.wait_ge(y_sum, 1)
            nc.scalar.copy(y, y_ps).then_inc(y_ready, 1)

        @block.vector
        def _(dve):
            dve.wait_ge(pad_zeroed, 1)
            seen = set()
            for step in STEPS:
                if step[0] == "table":
                    dve.wait_ge(table_high, 1)
                    nc.vector.tensor_tensor(table[:], table[:], table_parts[:, 0], ALU.subtract).then_inc(table_rest, 1)
                    dve.wait_ge(hot_ids_arrived, 16)
                    nc.vector.tensor_copy(hot_ids_16[:], hot_ids_in).then_inc(hot_ids_ready, 1)
                    dve.wait_ge(row_of_in, 16)
                elif step[0] == "onehot":
                    j = step[1]
                    dve.wait_ge(hot_ids_ready, 1)
                    if j >= KT // 2:
                        dve.wait_ge(onehot_used, j - KT // 2 + 1)
                    nc.vector.tensor_scalar(onehot[:, j % (KT // 2), :], hot_ids_16[:], row_of[:, j:j + 1], None,
                                            ALU.is_equal).then_inc(onehot_ready, 1)
                elif step[0] == "table low":
                    dve.wait_ge(table_mid, 1)
                    nc.vector.tensor_tensor(table_parts[:, 2], table[:], table_parts[:, 1],
                                            ALU.subtract).then_inc(table_low, 1)
                elif step[0] == "consts":
                    dve.wait_ge(consts_in, 16 * 3)
                    nc.vector.tensor_copy(ident_r[:], ident[:])
                    nc.vector.tensor_copy(pick[:], pick_in[:]).then_inc(pick_ready, 1)
                elif step[0] == "hot low":
                    dve.wait_ge(hot_high, 1)
                    nc.vector.tensor_tensor(e_low_t[:], e_blk[:, 0, :], e_high_t[:].bitcast(fp32),
                                            ALU.subtract).then_inc(hot_low, 1)
                elif step[0] == "weights":
                    i = step[1]
                    dve.wait_ge(w_high, i + 1)
                    nc.vector.tensor_tensor(w_parts[:, i % WBUF, 1, :], w_raw[:, i % WBUF, :],
                                            w_parts[:, i % WBUF, 0, :].bitcast(fp32), ALU.subtract).then_inc(w_low, 1)
                elif step[0] == "split":
                    f = step[1]
                    dve.wait_ge(e_high, f - Q + 1)
                    nc.vector.tensor_tensor(e_parts[:, f % EHL, :, :, 1, :], rows_twice(f),
                                            e_parts[:, f % EHL, :, :, 0, :].bitcast(fp32), ALU.subtract).then_inc(e_low, 1)
                elif step[0] == "chunk":
                    k = step[1]
                    tiles = CHUNKS[k][1]
                    first, n = tiles[0][0], len(tiles)
                    by = e_blk[:, first:first + 2, :]
                    if tiles[-1][0] == first:
                        by = e_blk[:, first:first + 1, :].to_broadcast([P, n, B])
                    dve.wait_ge(t_ready, k + 1)
                    for m in sorted({m for m, _ in tiles} - seen):
                        if m == 0:
                            dve.wait_ge(picked_out, 1)
                        else:
                            dve.wait_ge(spare_out, USE["block", m] + 1)
                        seen.add(m)
                    if k >= PRODS:
                        dve.wait_ge(summed, batch_of(FIRST_TILE[k - PRODS + 1] - 1) + 1)
                    nc.vector.tensor_tensor(prod[:, k % PRODS, 0:n, :], t_ps[k % TBUF][:, 0:n, :], by,
                                            ALU.mult).then_inc(prod_ready, 1)
                elif step[0] == "layer1" and step[1] > 0:
                    m = step[2]
                    dve.wait_ge(spare_filled, USE[step] + 1)
                    nc.vector.tensor_tensor(h1[:, m, :], spare[:], h1[:, m, :], ALU.add).then_inc(spare_out, 1)
            dve.wait_ge(spare_out, len(SPARE))
            for m in range(H1 // P):
                dve.wait_ge(h1_sum, m + 1)
                nc.vector.tensor_tensor(h1[:, m, :], h1_ps[m], h1[:, m, :], ALU.add).then_inc(h1_added, 1)

        @block.tensor
        def _(pe):
            batches = 0

            def sums(upto):
                nonlocal batches
                while batches < NBATCH and last_chunk_of(batches) < upto:
                    b = batches
                    pe.wait_ge(prod_ready, last_chunk_of(b) + 1)
                    per = ROWS_T // Q
                    if b == 0:
                        pe.wait_ge(hot_high, 1)
                    elif b % per == 0:
                        pe.wait_ge(z_out, b // per)
                    for t in range(Q * b, min(Q * b + Q, NT)):
                        k = next(k for k in range(len(CHUNKS)) if FIRST_TILE[k + 1] > t)
                        g, at = t % Q, Q * (b % per)
                        last = nc.tensor.matmul(z_ps[D * g:D * (g + 1), :], select[:, D - Q - at:2 * D - Q - at],
                                                prod[:, k % PRODS, t - FIRST_TILE[k], :],
                                                start=(b % per == 0), stop=(b % per == per - 1 or t + Q >= NT))
                    last.then_inc(summed, 1)
                    batches += 1

            def spare_free(step):
                if use_before(USE[step]) is not None:
                    pe.wait_ge(spare_out, use_before(USE[step]) + 1)

            stacks = 0
            top_waited = False
            for step in STEPS:
                if step[0] == "slice":
                    j = step[1]
                    if j == 0:
                        pe.wait_ge(table_low, 1)
                    pe.wait_ge(onehot_ready, j + 1)
                    for i in range(3):
                        for q in range(Q):
                            last = nc.tensor.matmul(z_ps[D * q:D * (q + 1), :], table_parts[:, i, q, j, :],
                                                    onehot[:, j % (KT // 2), q * B:(q + 1) * B],
                                                    start=(j == 0 and i == 0), stop=(j == J - 1 and i == 2))
                    last.then_inc(onehot_used, 1)
                elif step[0] == "feature" and step[1] < Q:
                    f = step[1]
                    if f == 0:
                        pe.wait_ge(pick_ready, 1)
                        pe.wait_ge(hot_low, 1)
                    spare_free(step)
                    rows = slice(D * (f % Q), D * (f % Q + 1))
                    nc.tensor.matmul(bank(step), pick[rows, 0, :], e_high_t[rows, :], start=True, stop=False)
                    nc.tensor.matmul(bank(step), pick[rows, 1, :], e_low_t[rows, :], start=False,
                                     stop=True).then_inc(spare_filled, 1)
                elif step[0] == "feature":
                    f = step[1]
                    pe.wait_ge(e_low, f - Q + 1)
                    spare_free(step)
                    for bt in range(BT):
                        parts = e_parts[:, f % EHL, bt].rearrange("p r s x -> p (r s x)")
                        last = nc.tensor.matmul(bank(step)[:, bt * P:(bt + 1) * P], parts, ident_r[:], start=True, stop=True)
                    last.then_inc(spare_filled, 1)
                elif step[0] == "block":
                    n = step[1]
                    fs = min(F - Q * n, Q)
                    spare_free(step)
                    for bt in range(BT):
                        last = nc.tensor.transpose(bank(step)[0:fs * D, bt * P:(bt + 1) * P],
                                                   e_nat[:, n % NAT, bt, 0:fs, :].rearrange("p f x -> p (f x)"), ident[:])
                    last.then_inc(spare_filled, 1)
                elif step[0] in ("product", "layer1"):
                    use, m = step[1:3]
                    operands = layer1_operands(use)
                    i = step[3] if step[0] == "product" else len(operands) - 1
                    cols = slice(m * P, (m + 1) * P)
                    if not top_waited:
                        pe.wait_ge(top_in, 16 * 7)
                        top_waited = True
                    if i == 0:
                        spare_free(("layer1", use, m))
                        pe.wait_ge(z_out, FLUSH[use])
                    weights, by = w1d[:, cols], dense[:]
                    if operands[i] >= 0:
                        weights, by = w1[:, operands[i], cols], z[:, operands[i], :]
                    last = nc.tensor.matmul(spare[:], weights, by, start=(i == 0), stop=(step[0] == "layer1"))
                    if step[0] == "layer1":
                        last.then_inc(spare_filled, 1)
                elif step[0] == "chunk":
                    k = step[1]
                    if k >= TBUF:
                        pe.wait_ge(prod_ready, k - TBUF + 1)
                    else:
                        uses = [n for n in range(EARLY) if bank_of(n) in (1 + 2 * k, 2 + 2 * k)]
                        if uses:
                            pe.wait_ge(spare_out, uses[-1] + 1)
                    part = FIRST_PART[k]
                    for n, (m, parts) in enumerate(CHUNKS[k][1]):
                        for at, (f, qs) in enumerate(parts):
                            i = part // PIECE
                            if part % PIECE == 0:
                                pe.wait_ge(w_loaded[i % WRING], 32 * (i // WRING + 1))
                            if USE["feature", f] + 1 > stacks:
                                stacks = USE["feature", f] + 1
                                pe.wait_ge(spare_out, stacks)
                            last = nc.tensor.matmul(t_ps[k % TBUF][:, n, :], w_ring[:, i % WRING, part % PIECE, :],
                                                    e_stack(f), start=(at == 0), stop=(at == len(parts) - 1))
                            part += 1
                    last.then_inc(t_ready, 1)
                    sums(k - TBUF + 1)
            sums(len(CHUNKS))

            pe.wait_ge(z_out, KT)
            for m in range(H1 // P):
                for kt in range(FLUSH[-1], KT):
                    last = nc.tensor.matmul(h1_ps[m], w1[:, kt, m * P:(m + 1) * P], z[:, kt, :],
                                            start=(kt == FLUSH[-1]), stop=(kt == KT - 1))
                last.then_inc(h1_sum, 1)
            for kt in range(H1 // P):
                pe.wait_ge(h1_ready, kt + 1)
                for m in range(H2 // P):
                    last = nc.tensor.matmul(h2_ps[m], w2[:, kt, m * P:(m + 1) * P], h1[:, kt, :],
                                            start=(kt == 0), stop=(kt == H1 // P - 1))
                    if kt == H1 // P - 1:
                        last.then_inc(h2_sum, 1)
            for m in range(H2 // P):
                pe.wait_ge(h2_ready, m + 1)
                last = nc.tensor.matmul(y_ps, w3[:, m:m + 1], h2[:, m, :], start=(m == 0), stop=(m == H2 // P - 1))
            last.then_inc(y_sum, 1)


def lay_out(inputs):
    import numpy as np

    def array(name):
        return np.ascontiguousarray(inputs[name])

    arrays = {f"tbl_{f}": array(f"tbl_{f}") for f in range(F)}
    ids = array("ids")[:, ORDER]
    arrays["hot_ids"] = np.ascontiguousarray(ids.T[:Q].reshape(1, Q * B))
    arrays["ids"] = np.ascontiguousarray(ids.reshape(BT, P, F).transpose(1, 2, 0)[:, Q:].reshape(P, -1))
    arrays["dense"] = np.ascontiguousarray(array("dense_ctx").T)
    w = array("L0_rec_w")
    parts = np.zeros((D, NPIECE * PIECE, Q, D), w.dtype)
    for n, (m, f, qs) in enumerate(PARTS):
        for q in qs:
            a, b = ORDER[f], ORDER[Q * m + q]
            parts[:, n, q, :] = w[:, pair_index(b, a), :] if b < a else w[:, pair_index(a, b), :].T
    arrays["w"] = np.ascontiguousarray(parts.reshape(D, NPIECE, Q * WC).transpose(1, 0, 2).reshape(NPIECE, P, WC))
    w1 = array("W_top1")
    w1_z = np.zeros((P, KT, H1), w1.dtype)
    for t, (m, parts_) in enumerate(TILES):
        kt = z_row(t, 0)[0]
        for f, qs in parts_:
            for q in qs:
                a, b = ORDER[f], ORDER[Q * m + q]
                w1_z[z_row(t, q)[1], kt] = w1[pair_index(min(a, b), max(a, b))]
    arrays["w1_z"] = w1_z
    arrays["w1_dense"] = np.ascontiguousarray(w1[NPAIR:])
    arrays["b1"] = np.ascontiguousarray(array("b_top1").reshape(H1 // P, P).T)
    arrays["w2"] = np.ascontiguousarray(array("W_top2").reshape(H1 // P, P, H2).transpose(1, 0, 2))
    arrays["b2"] = np.ascontiguousarray(array("b_top2").reshape(H2 // P, P).T)
    arrays["w3"] = np.ascontiguousarray(array("W_top3").reshape(H2 // P, P).T)
    arrays["ident"] = np.eye(P, dtype=np.float32)
    select = np.zeros((P, 2 * D - Q), np.float32)
    for q in range(Q):
        select[D * q:D * (q + 1), D - Q + q] = 1.0
    arrays["select"] = select
    arrays["hot_rows"] = np.arange(KH * J, dtype=np.float32).reshape(KH, J)
    pick = np.zeros((Q, D, 2, 2, 2, D), np.float32)
    for s in range(2):
        for x in range(D):
            pick[:, x, s, :, s, x] = 1.0
    arrays["pick"] = pick.reshape(P, 2, P)
    return arrays


def kernel(**inputs):
    import concourse.bacc as _bacc
    from concourse import mybir as _mybir
    from concourse.bass_utils import run_bass_kernel_spmd as _run

    nc = _bacc.Bacc("TRN2", target_bir_lowering=False, num_devices=1)
    arrays = {f"in_{name}": a for name, a in lay_out(inputs).items()}
    aps = {name: nc.dram_tensor(name, a.shape, _mybir.dt.from_np(a.dtype), kind="ExternalInput").ap()
           for name, a in arrays.items()}
    out = nc.dram_tensor("out_y", (B, 1), _mybir.dt.float32, kind="ExternalOutput").ap()
    tower(nc, aps["in_dense"], aps["in_ids"], [aps[f"in_tbl_{f}"] for f in range(F)],
          aps["in_hot_ids"], aps["in_hot_rows"], aps["in_pick"], aps["in_w"], aps["in_w1_z"],
          aps["in_w1_dense"], aps["in_b1"], aps["in_w2"], aps["in_b2"], aps["in_w3"], aps["in_ident"],
          aps["in_select"], out)
    r = _run(nc, [arrays], core_ids=[0])
    return r.results[0]["out_y"]
```
